# Optimizing a Trainium2 kernel written in Bass

```python
import numpy as np
import jax
import jax.numpy as jnp

def _softmax(x, axis=-1):
    return jax.nn.softmax(x, axis=axis)

def _gelu(x):
    return jax.nn.gelu(x, approximate=True)

def _silu(x):
    return jax.nn.silu(x)

def _sigmoid(x):
    return jax.nn.sigmoid(x)

def _layernorm(x, axis=-1, eps=1e-05):
    m = jnp.mean(x, axis=axis, keepdims=True)
    v = jnp.var(x, axis=axis, keepdims=True)
    return (x - m) / jnp.sqrt(v + eps)

def _scatter_add(tgt, idx, src, axis=0):
    return tgt.at[idx].add(src)

def _segment_sum(src, seg, n):
    return jax.ops.segment_sum(src, seg, n)
kernel_name = 'mk_decoder_preln_d1_seqx_r8_e000d5'

def setup_inputs(seed: int=0):
    np.random.seed(seed)
    _w = jnp.asarray

    def _rec_inputs():
        import jax
        import jax.numpy as jnp
        _rk = jax.random.key(seed)
        x = 7.22e-05 + 1 * jax.random.normal(jax.random.fold_in(_rk, 1), (8, 128, 256), jnp.float32)
        _lenS = 128 - jax.random.randint(jax.random.fold_in(_rk, 7), (8,), 0, max(1, 128 // 4) + 1, jnp.int32)
        _lenS2 = 128 - jax.random.randint(jax.random.fold_in(_rk, 8), (8,), 0, max(1, 128 // 4) + 1, jnp.int32)
        _ctx_1024P = jax.random.normal(jax.random.fold_in(_rk, 11), (8, 16, 128), jnp.float32)
        _ctx_1024c = jax.random.dirichlet(jax.random.fold_in(_rk, 511), 0.3 * jnp.ones((16,), jnp.float32), (8, 128))
        _ctx_1024t = jnp.einsum('bsk,bkd->bsd', _ctx_1024c, _ctx_1024P)
        _ctx_1024t = _ctx_1024t * jax.lax.rsqrt(jnp.mean(jnp.square(_ctx_1024t)) + 1e-12) * 0.953939
        ctx_1024 = -1.39393e-06 + 0.999914 * (_ctx_1024t + 0.3 * jax.random.normal(jax.random.fold_in(_rk, 611), (8, 128, 128), jnp.float32))
        fside_BxSx2_0 = jax.random.uniform(jax.random.fold_in(_rk, 12), (8, 128, 2), jnp.float32, 0.0, 0.999707)
        return (x, ctx_1024, fside_BxSx2_0)
    x, ctx_1024, fside_BxSx2_0 = _rec_inputs()

    def _L0_attn_setup():
        import jax, jax.numpy as jnp
        import numpy as np
        H = 16
        DK = 128
        DV = 128
        M = 64
        EPS = 1e-05
        CLAMP = 32.0
        ROPE_BASE = 10000.0

        def _rope(x, cos, sin):
            x1, x2 = jnp.split(x, 2, axis=-1)
            return jnp.concatenate([x1 * cos - x2 * sin, x2 * cos + x1 * sin], axis=-1)
        key = jax.random.key(seed)
        ks = jax.random.split(key, 9)
        B, T, D = (1, 256, 256)
        sc = 0.02
        return {'hidden_states': jax.random.normal(ks[0], (B, T, D), jnp.float32), 'Wq': jax.random.normal(ks[1], (H * DK, D), jnp.float32) * sc, 'Wk': jax.random.normal(ks[2], (H * DK, D), jnp.float32) * sc, 'Wv': jax.random.normal(ks[3], (H * DV, D), jnp.float32) * sc, 'Wg': jax.random.normal(ks[4], (H * DV, D), jnp.float32) * sc, 'Wo': jax.random.normal(ks[5], (D, H * DV), jnp.float32) * sc, 'Ws1': jax.random.normal(ks[6], (16, D), jnp.float32) * sc, 'Ws2': jax.random.normal(ks[7], (H * M, 16), jnp.float32) * sc, 'bs2': jnp.zeros((H * M,), jnp.float32), 'g_norm_weight': jnp.ones((DV,), jnp.float32)}
    _L0_attn_all = _L0_attn_setup()
    _L0_attn_in = {k: v for k, v in _L0_attn_all.items() if k in ('Wq', 'Wk', 'Wv', 'Wg', 'Wo', 'Ws1', 'Ws2', 'bs2', 'g_norm_weight')}
    del _L0_attn_all

    def _L0_xattn_setup():
        import jax, jax.numpy as jnp
        import numpy as np
        DIM = 256
        CTX_DIM = 128
        N_HEADS = 32
        HEAD_DIM = DIM // N_HEADS
        POS_DIM = 2
        B, N, CTXN = (2, 256, 256)
        ROPE_BASE = 10000.0

        def apply_axial_rope(x, pos):
            b, n, h, d = x.shape
            p = pos.shape[-1]
            dpa = d // p
            half = dpa // 2
            freqs = ROPE_BASE ** (-jnp.arange(half, dtype=x.dtype) / half)
            ang = pos[..., :, None] * freqs
            cos = jnp.cos(ang)[:, :, None, :, :]
            sin = jnp.sin(ang)[:, :, None, :, :]
            xr = x.reshape(b, n, h, p, half, 2)
            x1, x2 = (xr[..., 0], xr[..., 1])
            out = jnp.stack([x1 * cos - x2 * sin, x1 * sin + x2 * cos], axis=-1)
            return out.reshape(b, n, h, d)
        key = jax.random.key(seed)
        ks = jax.random.split(key, 8)
        x = jax.random.normal(ks[0], (B, N, DIM), jnp.float32)
        ctx = jax.random.normal(ks[1], (B, CTXN, CTX_DIM), jnp.float32)
        pos_map = jax.random.uniform(ks[2], (B, N, POS_DIM), jnp.float32)
        ctx_pos_map = jax.random.uniform(ks[3], (B, CTXN, POS_DIM), jnp.float32)
        Wq = jax.random.normal(ks[4], (DIM, DIM), jnp.float32) / np.sqrt(DIM)
        Wkv = jax.random.normal(ks[5], (CTX_DIM, 2 * DIM), jnp.float32) / np.sqrt(CTX_DIM)
        Wout = jax.random.normal(ks[6], (DIM, DIM), jnp.float32) / np.sqrt(DIM)
        bout = jnp.zeros((DIM,), jnp.float32)
        return {'x': x, 'ctx': ctx, 'pos_map': pos_map, 'ctx_pos_map': ctx_pos_map, 'Wq': Wq, 'Wkv': Wkv, 'Wout': Wout, 'bout': bout}
    _L0_xattn_all = _L0_xattn_setup()
    _L0_xattn_in = {k: v for k, v in _L0_xattn_all.items() if k in ('Wq', 'Wkv', 'Wout', 'bout')}
    del _L0_xattn_all

    def _L0_ffn_setup():
        import jax, jax.numpy as jnp
        import numpy as np
        BS, SLEN, DIM, HID, E, K = (2, 128, 256, 128, 8, 2)
        INIT_STD = 0.02
        key = jax.random.key(seed)
        ks = jax.random.split(key, 8)
        s = INIT_STD
        return {'x': jax.random.normal(ks[0], (BS, SLEN, DIM), jnp.float32), 'gate_w': jax.random.normal(ks[1], (E, DIM), jnp.float32) * s, 'w1': jax.random.normal(ks[2], (E, HID, DIM), jnp.float32) * s, 'w2': jax.random.normal(ks[3], (E, DIM, HID), jnp.float32) * s, 'w3': jax.random.normal(ks[4], (E, HID, DIM), jnp.float32) * s, 'sw1': jax.random.normal(ks[5], (HID, DIM), jnp.float32) * s, 'sw2': jax.random.normal(ks[6], (DIM, HID), jnp.float32) * s, 'sw3': jax.random.normal(ks[7], (HID, DIM), jnp.float32) * s}
    _L0_ffn_all = _L0_ffn_setup()
    _L0_ffn_in = {k: v for k, v in _L0_ffn_all.items() if k in ('gate_w', 'w1', 'w2', 'w3', 'sw1', 'sw2', 'sw3')}
    del _L0_ffn_all
    return {'x': x, 'ctx_1024': ctx_1024, 'fside_BxSx2_0': fside_BxSx2_0, 'L0_attn_Wq': _L0_attn_in['Wq'], 'L0_attn_Wk': _L0_attn_in['Wk'], 'L0_attn_Wv': _L0_attn_in['Wv'], 'L0_attn_Wg': _L0_attn_in['Wg'], 'L0_attn_Wo': _L0_attn_in['Wo'], 'L0_attn_Ws1': _L0_attn_in['Ws1'], 'L0_attn_Ws2': _L0_attn_in['Ws2'], 'L0_attn_bs2': _L0_attn_in['bs2'], 'L0_attn_g_norm_weight': _L0_attn_in['g_norm_weight'], 'L0_xattn_Wq': _L0_xattn_in['Wq'], 'L0_xattn_Wkv': _L0_xattn_in['Wkv'], 'L0_xattn_Wout': _L0_xattn_in['Wout'], 'L0_xattn_bout': _L0_xattn_in['bout'], 'L0_ffn_gate_w': _L0_ffn_in['gate_w'], 'L0_ffn_w1': _L0_ffn_in['w1'], 'L0_ffn_w2': _L0_ffn_in['w2'], 'L0_ffn_w3': _L0_ffn_in['w3'], 'L0_ffn_sw1': _L0_ffn_in['sw1'], 'L0_ffn_sw2': _L0_ffn_in['sw2'], 'L0_ffn_sw3': _L0_ffn_in['sw3']}

def reference(x, ctx_1024, fside_BxSx2_0, L0_attn_Wq, L0_attn_Wk, L0_attn_Wv, L0_attn_Wg, L0_attn_Wo, L0_attn_Ws1, L0_attn_Ws2, L0_attn_bs2, L0_attn_g_norm_weight, L0_xattn_Wq, L0_xattn_Wkv, L0_xattn_Wout, L0_xattn_bout, L0_ffn_gate_w, L0_ffn_w1, L0_ffn_w2, L0_ffn_w3, L0_ffn_sw1, L0_ffn_sw2, L0_ffn_sw3):
    import jax
    import jax.numpy as jnp

    def _L0_attn_ref(hidden_states, Wq, Wk, Wv, Wg, Wo, Ws1, Ws2, bs2, g_norm_weight):
        import jax, jax.numpy as jnp
        import numpy as np
        H = 16
        DK = 128
        DV = 128
        M = 64
        EPS = 1e-05
        CLAMP = 32.0
        ROPE_BASE = 10000.0

        def _rope(x, cos, sin):
            x1, x2 = jnp.split(x, 2, axis=-1)
            return jnp.concatenate([x1 * cos - x2 * sin, x2 * cos + x1 * sin], axis=-1)
        B, T, D = hidden_states.shape
        hs = hidden_states
        q = (hs @ Wq.T).reshape(B, T, H, DK)
        k = (hs @ Wk.T).reshape(B, T, H, DK)
        pos = jnp.arange(T, dtype=jnp.float32)
        inv_freq = 1.0 / ROPE_BASE ** (jnp.arange(0, DK, 2, dtype=jnp.float32) / DK)
        ang = pos[:, None] * inv_freq[None, :]
        cos = jnp.cos(ang)[None, :, None, :]
        sin = jnp.sin(ang)[None, :, None, :]
        q = _rope(q, cos, sin).transpose(0, 2, 1, 3)
        k = _rope(k, cos, sin).transpose(0, 2, 1, 3)
        v = (hs @ Wv.T).reshape(B, T, H, DV).transpose(0, 2, 1, 3)
        s = hs @ Ws1.T @ Ws2.T + bs2
        s = jnp.clip(s, -CLAMP, CLAMP).reshape(B, T, H, M).transpose(0, 2, 1, 3)
        z = jax.lax.cumlogsumexp(s, axis=2)
        es = jnp.exp(s)
        enz = jnp.exp(-z)
        scale = DK ** (-0.5)
        mask = jnp.tril(jnp.ones((T, T), dtype=bool))
        A = jnp.einsum('bhtd,bhjd->bhtj', q, k) * scale
        A = jnp.where(mask, A, 0.0)
        ok = enz * jnp.einsum('bhtj,bhjm->bhtm', A, es)
        qv = jax.nn.softmax(ok, axis=-1)
        W2 = jnp.einsum('bhtm,bhjm->bhtj', qv * enz, es)
        W2 = jnp.where(mask, W2, 0.0)
        o = jnp.einsum('bhtj,bhjd->bhtd', W2, v)
        o = o.transpose(0, 2, 1, 3)
        g = (hs @ Wg.T).reshape(B, T, H, DV)
        o_n = o * jax.lax.rsqrt(jnp.mean(o * o, axis=-1, keepdims=True) + EPS) * g_norm_weight
        o_g = o_n * (g * jax.nn.sigmoid(g))
        return o_g.reshape(B, T, H * DV) @ Wo.T

    def _L0_xattn_ref(x, ctx, pos_map, ctx_pos_map, Wq, Wkv, Wout, bout):
        import jax, jax.numpy as jnp
        import numpy as np
        DIM = 256
        CTX_DIM = 128
        N_HEADS = 32
        HEAD_DIM = DIM // N_HEADS
        POS_DIM = 2
        B, N, CTXN = (2, 256, 256)
        ROPE_BASE = 10000.0

        def apply_axial_rope(x, pos):
            b, n, h, d = x.shape
            p = pos.shape[-1]
            dpa = d // p
            half = dpa // 2
            freqs = ROPE_BASE ** (-jnp.arange(half, dtype=x.dtype) / half)
            ang = pos[..., :, None] * freqs
            cos = jnp.cos(ang)[:, :, None, :, :]
            sin = jnp.sin(ang)[:, :, None, :, :]
            xr = x.reshape(b, n, h, p, half, 2)
            x1, x2 = (xr[..., 0], xr[..., 1])
            out = jnp.stack([x1 * cos - x2 * sin, x1 * sin + x2 * cos], axis=-1)
            return out.reshape(b, n, h, d)
        b, n, _ = x.shape
        ctx_n = ctx.shape[1]
        q = (x @ Wq).reshape(b, n, N_HEADS, HEAD_DIM)
        k, v = jnp.split(ctx @ Wkv, 2, axis=-1)
        k = k.reshape(b, ctx_n, N_HEADS, HEAD_DIM)
        v = v.reshape(b, ctx_n, N_HEADS, HEAD_DIM)
        q = apply_axial_rope(q, pos_map)
        k = apply_axial_rope(k, ctx_pos_map)
        scale = 1.0 / np.sqrt(HEAD_DIM).astype(np.float32)
        logits = jnp.einsum('bqhd,bkhd->bhqk', q, k) * scale
        w = jax.nn.softmax(logits, axis=-1)
        attn = jnp.einsum('bhqk,bkhd->bqhd', w, v)
        attn = attn.reshape(b, n, N_HEADS * HEAD_DIM)
        return attn @ Wout + bout

    def _L0_ffn_ref(x, gate_w, w1, w2, w3, sw1, sw2, sw3):
        import jax, jax.numpy as jnp
        import numpy as np
        BS, SLEN, DIM, HID, E, K = (2, 128, 256, 128, 8, 2)
        INIT_STD = 0.02
        bs, slen, dim = x.shape
        xt = x.reshape(-1, dim)
        scores = jax.nn.sigmoid((xt @ gate_w.T).astype(jnp.float32))
        top_scores, sel = jax.lax.top_k(scores, K)
        flat_sel = sel.reshape(-1)
        order = jnp.argsort(flat_sel, stable=True)
        token_idx = order // K
        expert_sorted = flat_sel[order]
        slot_scores = top_scores.reshape(-1)[order]
        routed_x = xt[token_idx] * slot_scores[:, None].astype(xt.dtype)
        out_r = jnp.zeros_like(routed_x)
        for e in range(E):
            m = (expert_sorted == e)[:, None].astype(routed_x.dtype)
            h = jax.nn.silu(routed_x @ w1[e].T) * (routed_x @ w3[e].T)
            out_r = out_r + h @ w2[e].T * m
        shared = jax.nn.silu(xt @ sw1.T) * (xt @ sw3.T) @ sw2.T
        out = shared.at[token_idx].add(out_r)
        return out.reshape(bs, slen, dim)
    x = x + _L0_attn_ref(_layernorm(x, axis=-1), L0_attn_Wq, L0_attn_Wk, L0_attn_Wv, L0_attn_Wg, L0_attn_Wo, L0_attn_Ws1, L0_attn_Ws2, L0_attn_bs2, L0_attn_g_norm_weight)
    x = x + _L0_xattn_ref(_layernorm(x, axis=-1), ctx_1024, fside_BxSx2_0, fside_BxSx2_0, L0_xattn_Wq, L0_xattn_Wkv, L0_xattn_Wout, L0_xattn_bout)
    x = x + _L0_ffn_ref(_layernorm(x, axis=-1), L0_ffn_gate_w, L0_ffn_w1, L0_ffn_w2, L0_ffn_w3, L0_ffn_sw1, L0_ffn_sw2, L0_ffn_sw3)
    return x

_drawn_inputs = setup_inputs


def setup_inputs(seed=0):
    import zlib

    import numpy as np

    out = dict(_drawn_inputs(seed))
    spreads = {'L0_attn_bs2': (0.0, 0.8),
     'L0_attn_g_norm_weight': (1.0, 0.578),
     'L0_xattn_bout': (0.0, 0.1)}
    factors = {'L0_attn_Wq': 8.0,
     'L0_attn_Wk': 8.0,
     'L0_attn_Ws1': 8.0,
     'L0_attn_Ws2': 8.0,
     'L0_ffn_gate_w': 8.0,
     'L0_ffn_w1': 8.0,
     'L0_ffn_w2': 8.0,
     'L0_ffn_w3': 8.0,
     'L0_ffn_sw1': 5.614,
     'L0_ffn_sw2': 5.583,
     'L0_ffn_sw3': 5.547}
    for name, (base, spread) in spreads.items():
        noise = np.random.default_rng([zlib.crc32(name.encode()), seed]).standard_normal(out[name].shape)
        drawn = base * np.exp(spread * noise) if base else spread * noise
        out[name] = jnp.asarray(drawn.astype(out[name].dtype))
    for name, factor in factors.items():
        out[name] = (out[name] * factor).astype(out[name].dtype)
    return out
```

```python
from contextlib import ExitStack

import numpy as np

import concourse.bass as bass
from concourse import mybir

F32 = mybir.dt.float32
F32R = mybir.dt.float32r
ALU = mybir.AluOpType
ACT = mybir.ActivationFunctionType
AX = mybir.AxisListType

P = 128
SEQS, TOK, DIM = 8, 128, 256
KC = DIM // P
ALL = SEQS * TOK
HALF = ALL // 2
EPS = 1e-5

HEADS, DK, SLOTS = 16, 128, 64
PAIRS = HEADS // 2
GROUPS = SEQS // 2
CLAMP = 32.0
S_RANK = 16
QUAD = 32

C_TRI, C_TRIS, C_ID, C_COS, C_SIN, C_ONE, C_FREQ, C_BEFORE = 0, 128, 256, 384, 512, 640, 641, 645
C_ALL = C_BEFORE + 64


def constants():
    c = np.zeros((P, C_ALL), np.float32)
    j, t = np.arange(P)[:, None], np.arange(TOK)[None, :]
    c[:, C_TRI:C_TRI + TOK] = j <= t
    c[:, C_TRIS:C_TRIS + TOK] = (j <= t) * np.float32(DK ** -0.5)
    c[:, C_ID:C_ID + P] = np.eye(P)
    freq = (1.0 / 10000.0 ** (np.arange(0, DK, 2, dtype=np.float32) / np.float32(DK))).astype(np.float32)
    angle = (np.arange(TOK, dtype=np.float32)[None, :] * freq[:, None]).astype(np.float32)
    cos, sin = np.cos(angle.astype(np.float64)), np.sin(angle.astype(np.float64))
    c[:, C_COS:C_COS + TOK] = np.concatenate([cos, cos])
    c[:, C_SIN:C_SIN + TOK] = np.concatenate([sin, -sin])
    c[[S_RANK, QUAD + S_RANK], C_ONE] = 1.0
    c[:, C_FREQ:C_FREQ + 4] = [1.0, 10000.0 ** -0.5, 1.0, 10000.0 ** -0.5]
    e = np.arange(8)
    c[:, C_BEFORE:C_BEFORE + 64] = (e[None, :] < e[:, None]).astype(np.float32).reshape(1, 64)
    return c


FILLS = ([("QK", n) for n in range(8)] + [("VG", b) for b in range(4)] + [("ST", 0), ("ST", 1), ("SN", 0), ("SN", 1)]
         + [("VG", b) for b in range(4, 8)] + [("CS", 0), ("CS", 1)])
NFILL = len(FILLS)
NDRAIN = NFILL - 2
PLACE = {f: n for n, f in enumerate(FILLS)}
LEAD = 4


def at(i, g):
    return 4 * i + g + 1 + LEAD


def filled(r, f):
    return NFILL * r + PLACE[f] + 1


def drained(r, f):
    return NDRAIN * r + PLACE[f] + 1


PE_ORDER = [
    ("A", 0), ("QK", 0), ("A", 1), ("QK", 1), ("E", 0), ("QK", 2), ("A", 2), ("E", 1), ("QK", 3),
    ("A", 3), ("T", 0), ("QK", 4), ("E", 2), ("W", 0), ("T", 1), ("QK", 5), ("E", 3), ("W", 1), ("O", 0), ("QK", 6),
    ("T", 2), ("O", 1), ("QK", 7), ("W", 2), ("T", 3), ("VG", 0), ("O", 2), ("W", 3), ("OT", 0), ("VG", 1),
    ("O", 3), ("OT", 1), ("Y", 0), ("VG", 2), ("Y", 1), ("VG", 3), ("OT", 2), ("ST", 0), ("ST", 1),
    ("OT", 3), ("SN", 0), ("SN", 1), ("Y", 2), ("VG", 4), ("Y", 3), ("VG", 5), ("VG", 6), ("VG", 7), ("CS", 0), ("CS", 1)]
DVE_ORDER = [
    ("A", 0), ("QK", 0), ("A", 1), ("QK", 1), ("E", 0), ("QK", 2), ("A", 2), ("SUM", 0), ("E", 1), ("QK", 3),
    ("A", 3), ("SUM", 1), ("QK", 4), ("W", 0), ("E", 2), ("QK", 5), ("W", 1), ("SUM", 2), ("E", 3), ("QK", 6),
    ("MS", 0), ("SUM", 3), ("QK", 7), ("O", 0), ("MS", 1), ("W", 2), ("VG", 0), ("O", 1), ("W", 3), ("VG", 1),
    ("MS", 2), ("Y", 0), ("VG", 2), ("MS", 3), ("O", 2), ("Y", 1), ("VG", 3), ("O", 3), ("ST", 0), ("ST", 1),
    ("SN", 0), ("SN", 1), ("Y", 2), ("VG", 4), ("Y", 3), ("VG", 5), ("VG", 6), ("VG", 7)]
ACT_ORDER = [
    ("W2P", 0), ("VGHI", 0), ("E", 0), ("E", 1), ("T", 0), ("E", 2), ("T", 1), ("E", 3), ("O", 0),
    ("T", 2), ("O", 1), ("T", 3), ("VG", 0), ("QKHI", 0), ("O", 2), ("OT", 0), ("VG", 1), ("O", 3), ("OT", 1), ("VG", 2),
    ("VG", 3), ("OT", 2), ("ST", 0), ("ST", 1), ("OT", 3), ("SN", 0), ("SN", 1),
    ("VG", 4), ("VG", 5), ("VG", 6), ("VG", 7), ("CS", 0), ("CS", 1)]
POOL_ORDER = [
    ("QK", 0), ("QK", 1), ("VGLO", 0), ("QK", 2), ("E", 0), ("QK", 3), ("E", 1), ("QK", 4), ("QK", 5), ("E", 2), ("QK", 6),
    ("E", 3), ("QK", 7), ("MS", 0), ("MS", 1), ("QKLO", 0), ("MS", 2), ("MS", 3)]
PROJECTING = {"QK", "VG", "ST", "SN", "CS", "W2P", "VGHI", "VGLO", "QKHI", "QKLO"}


def turns(order, i, attend, project, split_qk, split_vg):
    for step, n in order:
        if step in ("QKHI", "QKLO") and not split_qk or step in ("VGHI", "VGLO") and not split_vg:
            continue
        if (project if step in PROJECTING else attend):
            yield step, n


def every_turn(engine, run):
    run(-1, attend=False, project=True, split_qk=True, split_vg=False)
    with engine.Fori(0, PAIRS - 2) as i:
        run(i, attend=True, project=True, split_qk=True, split_vg=True)
    run(PAIRS - 2, attend=True, project=True, split_qk=False, split_vg=True)
    run(PAIRS - 1, attend=True, project=False, split_qk=False, split_vg=False)


def split_product(pe, out, w_hi, w_lo, m_hi, m_lo, first=True, last=True):
    pe.matmul(out, w_hi, m_hi, start=first, stop=False)
    pe.matmul(out, w_hi, m_lo, start=False, stop=False)
    return pe.matmul(out, w_lo, m_hi, start=False, stop=last)


def bank(ps, a, b, k):
    return ps[:, a:b].rearrange("p (k c) -> p k c", k=k)


class Norm:

    def __init__(self, nc, ctx, banks, xs, hn, ht_hi, ht_lo, ident, name):
        sb = lambda n, s: ctx.enter_context(nc.sbuf_tensor(f"{name}_{n}", s, F32))
        sem = lambda n: ctx.enter_context(nc.semaphore(f"{name}_{n}"))
        self.banks, self.xs, self.hn, self.ht_hi, self.ht_lo, self.ident = banks, xs, hn, ht_hi, ht_lo, ident
        self.stats, self.mv = sb("stats", [P, SEQS, 6]), sb("mv", [P, SEQS, 2])
        self.var_eps, self.rstd, self.minus_half = sb("var_eps", [P, SEQS]), sb("rstd", [P, SEQS]), sb("minus_half", [P, SEQS])
        self.stats_done, self.mv_done, self.var_done = sem("stats_done"), sem("mv_done"), sem("var_done")
        self.half_set, self.rstd_done, self.hn_done = sem("half_set"), sem("rstd_done"), sem("hn_done")
        self.turned, self.hi_done, self.lo_done = sem("turned"), sem("hi_done"), sem("lo_done")

    def vector_norm(self, dve, x_in=None):
        for b in range(SEQS):
            if x_in is not None and b % 4 == 0:
                dve.wait_ge(x_in[b // 4], 16)
            dve.bn_stats(out=self.stats[:, b, :], in_=self.xs[:, b, :]).then_inc(self.stats_done, 1)
        for b in range(SEQS):
            dve.wait_ge(self.stats_done, b + 1)
            dve.bn_aggr(out=self.mv[:, b, :], in_=self.stats[:, b, :]).then_inc(self.mv_done, 1)
        dve.wait_ge(self.mv_done, SEQS)
        dve.tensor_scalar(self.var_eps[:, :], self.mv[:, :, 1], EPS, None, ALU.add).then_inc(self.var_done, 1)
        dve.wait_ge(self.rstd_done, 1)
        for b in range(SEQS):
            dve.tensor_scalar(self.hn[:, b, :], self.xs[:, b, :], self.mv[:, b, 0:1], self.rstd[:, b:b + 1],
                              ALU.subtract, ALU.mult).then_inc(self.hn_done, 1)

    def pool(self, pool):
        pool.memset(self.minus_half[:, :], -0.5).then_inc(self.half_set, 1)
        pool.wait_ge(self.half_set, 1)
        pool.wait_ge(self.var_done, 1)
        pool.tensor_tensor(self.rstd[:, :], self.var_eps[:, :], self.minus_half[:, :], ALU.pow).then_inc(self.rstd_done, 1)

    def tensor(self, pe):
        for half in range(2):
            pe.wait_ge(self.hn_done, 4 * half + 4)
            for kc in range(KC):
                for b in range(4):
                    mm = pe.transpose(self.banks[2 * half + kc][:, b * TOK:(b + 1) * TOK],
                                      self.hn[:, 4 * half + b, kc * P:(kc + 1) * P], self.ident)
                mm.then_inc(self.turned, 1)

    def scalar(self, act):
        for n in range(4):
            half, kc = n // 2, n % 2
            act.wait_ge(self.turned, n + 1)
            act.activation(self.ht_hi[:, kc, half * HALF:(half + 1) * HALF], self.banks[n][:, :], ACT.Copy).then_inc(self.hi_done, 1)

    def vector_low(self, dve):
        for n in range(4):
            half, kc = n // 2, n % 2
            cols = slice(half * HALF, (half + 1) * HALF)
            dve.wait_ge(self.hi_done, n + 1)
            dve.tensor_tensor(self.ht_lo[:, kc, cols], self.banks[n][:, :], self.ht_hi[:, kc, cols].bitcast(F32),
                              ALU.subtract).then_inc(self.lo_done, 1)


def slot_attention(nc, banks, xs, hn, ht_hi, ht_lo, con, x_in, a):
    tri, tris = con[:, C_TRI:C_TRI + TOK], con[:, C_TRIS:C_TRIS + TOK]
    ident, cos, sin = con[:, C_ID:C_ID + P], con[:, C_COS:C_COS + TOK], con[:, C_SIN:C_SIN + TOK]

    with ExitStack() as ctx:
        def sb(name, shape, dt=F32):
            return ctx.enter_context(nc.sbuf_tensor("sa_" + name, shape, dt))

        def sem(name):
            return ctx.enter_context(nc.semaphore("sa_" + name))

        qk_raw, vg_raw = sb("qk_raw", [P, KC, 512]), sb("vg_raw", [P, KC, 512])
        qk_hi, qk_lo = sb("qk_hi", [P, KC, 512], F32R), sb("qk_lo", [P, KC, 512], F32R)
        vg_hi, vg_lo = sb("vg_hi", [P, KC, 512], F32R), sb("vg_lo", [P, KC, 512], F32R)
        wo = sb("wo", [P, HEADS, DIM])
        gnorm = sb("gnorm", [P, 1])
        ws1_raw, ws1_hi, ws1_lo = sb("ws1_raw", [P, KC, P]), sb("ws1_hi", [P, KC, P], F32R), sb("ws1_lo", [P, KC, P], F32R)
        ws2_raw, ws2, ws2_pair = sb("ws2_raw", [P, PAIRS, P]), sb("ws2", [P, PAIRS, P], F32R), sb("ws2_pair", [P, P], F32R)
        u_full, us = sb("u_full", [P, ALL]), sb("us", [P, ALL], F32R)
        rope_cos, rope_sin = sb("rope_cos", [P, 2, HALF]), sb("rope_sin", [P, 2, HALF])
        qt, kt = sb("qt", [P, 2, ALL]), sb("kt", [P, 2, ALL])
        v, gate, th = sb("v", [P, SEQS, 2 * DK]), sb("gate", [P, SEQS, 2 * DK]), sb("th", [P, 2, 2 * DK])
        st, sn = sb("st", [P, 2, HALF]), sb("sn", [P, 2, HALF])
        es, es_t = sb("es", [P, SEQS, 2 * SLOTS]), sb("es_t", [P, 2, ALL])
        log_cs, enz = sb("log_cs", [P, 2, HALF]), sb("enz", [P, SEQS, 2 * SLOTS])
        att, okb, ex = sb("att", [P, 2, 4, TOK]), sb("okb", [P, 2, 4, SLOTS]), sb("ex", [P, 2, 4, SLOTS])
        qe, qet, w2t = sb("qe", [P, 2, 4, SLOTS]), sb("qet", [P, 2, 2, TOK]), sb("w2t", [P, 2, 4, TOK])
        og, ogt, junk = sb("og", [P, 2, 4, DK]), sb("ogt", [P, 2, 4, TOK]), sb("junk", [P, 4, DK])
        top, total, eps_t2 = sb("top", [P, 2, 4]), sb("total", [P, 4, 4]), sb("eps_t2", [P, 4, 4])
        ss, msq, rms = sb("ss", [P, 2, 4]), sb("msq", [P, 2, 4]), sb("rms", [P, 2, 4])
        minus_half = sb("minus_half", [P, 4])

        norm = Norm(nc, ctx, banks, xs, hn, ht_hi, ht_lo, ident, "norm1")
        con_in, ws1_in, ws2_in, gnorm_in, wo_in = sem("con_in"), sem("ws1_in"), sem("ws2_in"), sem("gnorm_in"), sem("wo_in")
        qk_in, vg_in = sem("qk_in"), sem("vg_in")
        ws1_hi_done, ws1_lo_done, ws2_hi_done, ws2_done = sem("ws1_hi_done"), sem("ws1_lo_done"), sem("ws2_hi_done"), sem("ws2_done")
        qk_hi_done, qk_lo_done, vg_hi_done, vg_lo_done = sem("qk_hi_done"), sem("qk_lo_done"), sem("vg_hi_done"), sem("vg_lo_done")
        u_ready, u_full_done, u_hi_done, us_done = sem("u_ready"), sem("u_full_done"), sem("u_hi_done"), sem("us_done")
        wo_scaled, zeros_set, half_set, pair_done = sem("wo_scaled"), sem("zeros_set"), sem("half_set"), sem("pair_done")
        fill, drain, summed = sem("fill"), sem("drain"), sem("summed")
        rope_parts, roped, v_done, th_done = sem("rope_parts"), sem("roped"), sem("v_done"), sem("th_done")
        es_t_done, es_done, log_done, enz_done = sem("es_t_done"), sem("es_done"), sem("log_done"), sem("enz_done")
        a_ready, e_ready, t_ready, w_ready = sem("a_ready"), sem("e_ready"), sem("t_ready"), sem("w_ready")
        o_ready, ot_ready, y_ready = sem("o_ready"), sem("ot_ready"), sem("y_ready")
        masked, scaled, topped, shifted = sem("masked"), sem("scaled"), sem("topped"), sem("shifted")
        totalled, eps_done, w2_done, msq_done = sem("totalled"), sem("eps_done"), sem("w2_done"), sem("msq_done")
        og_done, added = sem("og_done"), sem("added")
        exp_done, qet_done, squared, ogt_done = sem("exp_done"), sem("qet_done"), sem("squared"), sem("ogt_done")
        qe_done, rms_done = sem("qe_done"), sem("rms_done")

        fills = banks[0:2]
        ps_a, ps_e, ps_t, ps_w, ps_y = banks[2], banks[3], banks[4], banks[5], banks[3]
        ps_o = banks[6:8]

        block = ctx.enter_context(nc.Block())

        @block.sync
        def _(sp):
            sp.dma_start(xs[:, 0:4, :], a["x"][0:4].rearrange("b t d -> t b d")).then_inc(x_in[0], 16)
            sp.dma_start(con[:, :], a["constants"]).then_inc(con_in, 16)
            sp.dma_start(xs[:, 4:8, :], a["x"][4:8].rearrange("b t d -> t b d")).then_inc(x_in[1], 16)
            sp.dma_start(ws1_raw[:, :, :], a["ws1"]).then_inc(ws1_in, 16)
            sp.dma_start(qk_raw[:, :, :], a["wqk"][0]).then_inc(qk_in, 16)
            sp.dma_start(ws2_raw[:, :, :], a["ws2"]).then_inc(ws2_in, 16)
            sp.dma_start(vg_raw[:, :, :], a["wvg"][0]).then_inc(vg_in, 16)
            sp.dma_start(gnorm[:, :], a["g_norm"]).then_inc(gnorm_in, 16)
            sp.dma_start(wo[:, :, :], a["wo"]).then_inc(wo_in, 16)
            sp.wait_ge(qk_lo_done, 1)
            sp.dma_start(qk_raw[:, :, :], a["wqk"][1]).then_inc(qk_in, 16)
            sp.wait_ge(vg_lo_done, 1)
            sp.dma_start(vg_raw[:, :, :], a["wvg"][1]).then_inc(vg_in, 16)
            with sp.Fori(0, PAIRS - 2) as i:
                sp.wait_ge(vg_lo_done, i + 2)
                sp.dma_start(vg_raw[:, :, :], a["wvg"][i + 2]).then_inc(vg_in, 16)
                sp.wait_ge(qk_lo_done, i + 2)
                sp.dma_start(qk_raw[:, :, :], a["wqk"][i + 2]).then_inc(qk_in, 16)

        @block.tensor
        def _(pe):
            for s in (a_ready, e_ready, t_ready, w_ready, o_ready, ot_ready, y_ready):
                pe.sem_inc(s, LEAD)
            pe.wait_ge(con_in, 16)
            norm.tensor(pe)
            pe.wait_ge(norm.hi_done, 4)
            pe.wait_ge(norm.lo_done, 4)
            pe.wait_ge(ws1_lo_done, 1)
            for half in range(2):
                cols = slice(half * HALF, (half + 1) * HALF)
                for kc in range(KC):
                    mm = split_product(pe, banks[4 + half][:, :], ws1_hi[:, kc, :], ws1_lo[:, kc, :],
                                       ht_hi[:, kc, cols], ht_lo[:, kc, cols], kc == 0, kc == KC - 1)
                mm.then_inc(u_ready, 1)

            def run(i, attend, project, split_qk, split_vg):
                r = i + 1
                for step, n in turns(PE_ORDER, i, attend, project, split_qk, split_vg):
                    g = n
                    if step in PROJECTING:
                        place = PLACE[step, n]
                        ps = fills[place % 2]
                        if place >= 2:
                            pe.wait_ge(drain, NDRAIN * r + place - 1)
                        elif attend:
                            pe.wait_ge(summed, 2 * r - 1 + place)
                    if step == "A":
                        if g % 2 == 0:
                            pe.wait_ge(roped, 8 * i + 4 * (g // 2) + 4)
                        pe.wait_ge(masked, at(i, g - 1))
                        for u in range(4):
                            b, h = 2 * g + u // 2, u % 2
                            mm = pe.matmul(ps_a[:, u * TOK:(u + 1) * TOK], kt[:, h, b * TOK:(b + 1) * TOK],
                                           qt[:, h, b * TOK:(b + 1) * TOK], start=True, stop=True)
                        mm.then_inc(a_ready, 1)
                    elif step == "E":
                        pe.wait_ge(masked, at(i, g))
                        pe.wait_ge(scaled, at(i, g - 1))
                        if g == 0:
                            pe.wait_ge(added, at(i, -1))
                        for u in range(4):
                            b, h = 2 * g + u // 2, u % 2
                            mm = pe.matmul(ps_e[:, u * SLOTS:(u + 1) * SLOTS], att[:, g % 2, u, :],
                                           es[:, b, h * SLOTS:(h + 1) * SLOTS], start=True, stop=True)
                        mm.then_inc(e_ready, 1)
                    elif step == "T":
                        pe.wait_ge(qe_done, at(i, g))
                        if g == 0:
                            pe.wait_ge(ogt_done, at(i, -1))
                        else:
                            pe.wait_ge(qet_done, at(i, g - 1))
                        for b in range(2):
                            mm = pe.transpose(ps_t[:, b * TOK:(b + 1) * TOK],
                                              qe[:, g % 2, 2 * b:2 * b + 2, :].rearrange("p h m -> p (h m)"), ident)
                        mm.then_inc(t_ready, 1)
                    elif step == "W":
                        pe.wait_ge(qet_done, at(i, g))
                        pe.wait_ge(w2_done, at(i, g - 1))
                        for u in range(4):
                            b, h = 2 * g + u // 2, u % 2
                            mm = pe.matmul(ps_w[:, u * TOK:(u + 1) * TOK], es_t[:, h, b * TOK:(b + 1) * TOK],
                                           qet[:, g % 2, u // 2, :], start=True, stop=True)
                        mm.then_inc(w_ready, 1)
                    elif step == "O":
                        pe.wait_ge(w2_done, at(i, g))
                        pe.wait_ge(v_done, 8 * i + 2 * g + 2)
                        pe.wait_ge(og_done, at(i, g - 2))
                        for u in range(4):
                            b, h = 2 * g + u // 2, u % 2
                            mm = pe.matmul(ps_o[g % 2][:, u * DK:(u + 1) * DK], w2t[:, g % 2, u, :],
                                           v[:, b, h * DK:(h + 1) * DK], start=True, stop=True)
                        mm.then_inc(o_ready, 1)
                    elif step == "OT":
                        pe.wait_ge(og_done, at(i, g))
                        if g == 0:
                            pe.wait_ge(qet_done, at(i, 3))
                        else:
                            pe.wait_ge(ogt_done, at(i, g - 1))
                        for u in range(4):
                            mm = pe.transpose(ps_t[:, u * TOK:(u + 1) * TOK], og[:, g % 2, u, :], ident)
                        mm.then_inc(ot_ready, 1)
                    elif step == "Y":
                        pe.wait_ge(ogt_done, at(i, g))
                        pe.wait_ge(added, at(i, g - 1))
                        if g == 0:
                            pe.wait_ge(scaled, at(i, 3))
                        for b in range(2):
                            for h in range(2):
                                mm = pe.matmul(ps_y[:, b * DIM:(b + 1) * DIM], ogt[:, g % 2, 2 * b + h, :],
                                               wo[:, 2 * i + h, :], start=(h == 0), stop=(h == 1))
                        mm.then_inc(y_ready, 1)
                    elif step == "QK":
                        c, j = n // 4, n % 4
                        if n == 0:
                            pe.wait_ge(qk_lo_done, r + 1)
                        cols, w = slice(c * HALF, (c + 1) * HALF), slice(j * DK, (j + 1) * DK)
                        for kc in range(KC):
                            mm = split_product(pe, ps[:, :], qk_hi[:, kc, w], qk_lo[:, kc, w],
                                               ht_hi[:, kc, cols], ht_lo[:, kc, cols], kc == 0, kc == KC - 1)
                        mm.then_inc(fill, 1)
                    elif step == "VG":
                        if n == 0:
                            pe.wait_ge(vg_lo_done, r + 1)
                        cols = slice(n * TOK, (n + 1) * TOK)
                        for kc in range(KC):
                            mm = split_product(pe, ps[:, :], ht_hi[:, kc, cols], ht_lo[:, kc, cols],
                                               vg_hi[:, kc, :], vg_lo[:, kc, :], kc == 0, kc == KC - 1)
                        mm.then_inc(fill, 1)
                    elif step == "ST":
                        pe.wait_ge(pair_done, r + 1)
                        pe.matmul(ps[:, :], ws2_pair[:, :], us[:, n * HALF:(n + 1) * HALF],
                                  start=True, stop=True).then_inc(fill, 1)
                    elif step == "SN":
                        for b in range(4):
                            mm = pe.matmul(ps[:, b * P:(b + 1) * P], us[:, (4 * n + b) * TOK:(4 * n + b + 1) * TOK],
                                           ws2_pair[:, :], start=True, stop=True)
                        mm.then_inc(fill, 1)
                    elif step == "CS":
                        pe.wait_ge(es_done, 2 * r + n + 1)
                        pe.matmul(ps[:, :], tri, es[:, 4 * n:4 * n + 4, :].rearrange("p b m -> p (b m)"),
                                  start=True, stop=True).then_inc(fill, 1)

            pe.wait_ge(us_done, 4)
            pe.wait_ge(wo_scaled, 1)
            every_turn(pe, run)

        @block.vector
        def _(dve):
            for s in (masked, scaled, topped, shifted, totalled, eps_done, w2_done, msq_done, og_done, added):
                dve.sem_inc(s, LEAD)
            dve.memset(es_t[0:64, 1, :], 0.0).then_inc(zeros_set, 1)
            dve.memset(es_t[64:128, 0, :], 0.0).then_inc(zeros_set, 1)
            norm.vector_norm(dve, x_in)
            dve.wait_ge(ws1_hi_done, 1)
            dve.tensor_tensor(ws1_lo[:, :, :], ws1_raw[:, :, :], ws1_hi[:, :, :].bitcast(F32), ALU.subtract).then_inc(ws1_lo_done, 1)
            norm.vector_low(dve)
            dve.wait_ge(ws2_hi_done, 1)
            for q in (1, 3):
                rows = slice(q * QUAD, (q + 1) * QUAD)
                dve.tensor_tensor(ws2[rows, :, :], ws2_raw[rows, :, :], ws2[rows, :, :].bitcast(F32), ALU.subtract).then_inc(ws2_done, 1)
            for half in range(2):
                cols = slice(half * HALF, (half + 1) * HALF)
                dve.wait_ge(u_ready, half + 1)
                dve.wait_ge(con_in, 16)
                dve.tensor_scalar(u_full[:, cols], banks[4 + half][:, :], con[:, C_ONE:C_ONE + 1], None, ALU.add).then_inc(u_full_done, 1)
                dve.wait_ge(u_full_done, half + 1)
                dve.tensor_copy(us[:, cols], u_full[:, cols]).then_inc(us_done, 1)
                dve.wait_ge(us_done, 2 * half + 1)
                dve.tensor_tensor(us[64:128, cols], u_full[64:128, cols], us[64:128, cols].bitcast(F32), ALU.subtract).then_inc(us_done, 1)
            dve.wait_ge(wo_in, 16)
            dve.wait_ge(gnorm_in, 16)
            dve.tensor_scalar(wo[:, :, :], wo[:, :, :], gnorm[:, 0:1], 0.5, ALU.mult, ALU.mult).then_inc(wo_scaled, 1)

            def run(i, attend, project, split_qk, split_vg):
                r = i + 1
                for step, n in turns(DVE_ORDER, i, attend, project, split_qk, split_vg):
                    g, s = n, n % 2
                    if step in PROJECTING:
                        ps = fills[PLACE[step, n] % 2]
                        dve.wait_ge(fill, filled(r, (step, n)))
                    if step == "A":
                        dve.wait_ge(a_ready, at(i, g))
                        dve.wait_ge(e_ready, at(i, g - 2))
                        dve.tensor_tensor(att[:, s, :, :], bank(ps_a, 0, 512, 4),
                                          tris.unsqueeze(1).to_broadcast([P, 4, TOK]), ALU.mult).then_inc(masked, 1)
                    elif step == "E":
                        dve.wait_ge(e_ready, at(i, g))
                        dve.wait_ge(enz_done, 2 * i + g // 2 + 1)
                        dve.wait_ge(exp_done, at(i, g - 2))
                        dve.tensor_tensor(okb[:, s, :, :], bank(ps_e, 0, 256, 4),
                                          enz[:, 2 * g:2 * g + 2, :].rearrange("p b (h m) -> p (b h) m", h=2), ALU.mult).then_inc(scaled, 1)
                        dve.wait_ge(scaled, at(i, g))
                        dve.tensor_reduce(top[:, s, :], okb[:, s, :, :], AX.X, ALU.max).then_inc(topped, 1)
                        dve.wait_ge(topped, at(i, g))
                        dve.tensor_tensor(okb[:, s, :, :], okb[:, s, :, :],
                                          top[:, s, :].unsqueeze(2).to_broadcast([P, 4, SLOTS]), ALU.subtract).then_inc(shifted, 1)
                    elif step == "SUM":
                        dve.wait_ge(exp_done, at(i, g))
                        dve.tensor_reduce(total[:, g, :], ex[:, s, :, :], AX.X, ALU.add).then_inc(totalled, 1)
                        dve.wait_ge(totalled, at(i, g))
                        dve.wait_ge(msq_done, at(i, g - 4))
                        dve.scalar_tensor_tensor(out=eps_t2[:, g, :], in0=total[:, g, :], scalar=EPS, in1=total[:, g, :],
                                                 op0=ALU.mult, op1=ALU.mult).then_inc(eps_done, 1)
                    elif step == "W":
                        dve.wait_ge(w_ready, at(i, g))
                        dve.wait_ge(o_ready, at(i, g - 2))
                        dve.tensor_tensor(w2t[:, s, :, :], bank(ps_w, 0, 512, 4),
                                          tri.unsqueeze(1).to_broadcast([P, 4, TOK]), ALU.mult).then_inc(w2_done, 1)
                    elif step == "MS":
                        dve.wait_ge(squared, at(i, g))
                        dve.wait_ge(eps_done, at(i, g))
                        dve.wait_ge(rms_done, at(i, g - 2))
                        dve.scalar_tensor_tensor(out=msq[:, s, :], in0=ss[:, s, :], scalar=1.0 / DK, in1=eps_t2[:, g, :],
                                                 op0=ALU.mult, op1=ALU.add).then_inc(msq_done, 1)
                    elif step == "O":
                        dve.wait_ge(rms_done, at(i, g))
                        dve.wait_ge(drain, drained(i, ("VG", 2 * g + 1)))
                        dve.wait_ge(ot_ready, at(i, g - 2))
                        for u in range(4):
                            b, h = 2 * g + u // 2, u % 2
                            ins = dve.scalar_tensor_tensor(out=og[:, s, u, :], in0=ps_o[s][:, u * DK:(u + 1) * DK],
                                                           scalar=rms[:, s, u:u + 1], in1=gate[:, b, h * DK:(h + 1) * DK],
                                                           op0=ALU.mult, op1=ALU.mult)
                        ins.then_inc(og_done, 1)
                    elif step == "Y":
                        dve.wait_ge(y_ready, at(i, g))
                        dve.wait_ge(added, at(i, g - 1))
                        dve.tensor_tensor(xs[:, 2 * g:2 * g + 2, :], bank(ps_y, 0, 512, 2), xs[:, 2 * g:2 * g + 2, :],
                                          ALU.add).then_inc(added, 1)
                    elif step == "QK":
                        if attend or n >= 2:
                            dve.wait_ge(roped, 8 * r + n - 1)
                        cos4 = cos.unsqueeze(1).to_broadcast([P, 4, TOK])
                        sin4 = sin.unsqueeze(1).to_broadcast([P, 4, TOK])
                        psv = bank(ps, 0, 512, 4)
                        rs = rope_sin[:, s, :].rearrange("p (b t) -> p b t", b=4)
                        dve.tensor_tensor(rope_cos[:, s, :].rearrange("p (b t) -> p b t", b=4), psv, cos4, ALU.mult)
                        dve.tensor_tensor(rs[0:64], psv[64:128], sin4[64:128], ALU.mult)
                        dve.tensor_tensor(rs[64:128], psv[0:64], sin4[0:64], ALU.mult).then_inc(drain, 1)
                    elif step == "VG":
                        dve.wait_ge(th_done, 8 * r + n + 1)
                        if attend:
                            dve.wait_ge(og_done, at(i, n // 2))
                        dve.scalar_tensor_tensor(out=gate[:, n, :], in0=th[:, s, :], scalar=1.0, in1=ps[:, 256:512],
                                                 op0=ALU.add, op1=ALU.mult).then_inc(drain, 1)
                    elif step in ("ST", "SN"):
                        dst, done = (st, es_t_done) if step == "ST" else (sn, es_done)
                        if attend:
                            dve.wait_ge(done, 2 * r + n - 1)
                        dve.tensor_scalar(dst[:, n, :], ps[:, :], -CLAMP, CLAMP, ALU.max, ALU.min).then_inc(drain, 1)

            every_turn(dve, run)

        @block.scalar
        def _(act):
            for s in (exp_done, qet_done, squared, ogt_done):
                act.sem_inc(s, LEAD)
            act.wait_ge(ws1_in, 16)
            act.activation(ws1_hi[:, :, :], ws1_raw[:, :, :], ACT.Copy).then_inc(ws1_hi_done, 1)
            act.wait_ge(qk_in, 16)
            act.activation(qk_hi[:, :, :], qk_raw[:, :, :], ACT.Copy).then_inc(qk_hi_done, 1)
            norm.scalar(act)
            act.wait_ge(ws2_in, 16)
            act.activation(ws2[:, :, :], ws2_raw[:, :, :], ACT.Copy).then_inc(ws2_hi_done, 1)
            act.wait_ge(vg_in, 16)
            act.activation(vg_hi[:, :, :], vg_raw[:, :, :], ACT.Copy).then_inc(vg_hi_done, 1)
            act.wait_ge(ws2_done, 2)

            def run(i, attend, project, split_qk, split_vg):
                r = i + 1
                for step, n in turns(ACT_ORDER, i, attend, project, split_qk, split_vg):
                    g, s = n, n % 2
                    if (step, n) == ("CS", 0):
                        act.preload_act_table_set("natural_log_exp_and_others")
                    if step in ("VG", "CS"):
                        ps = fills[PLACE[step, n] % 2]
                        act.wait_ge(fill, filled(r, (step, n)))
                    if step == "W2P":
                        if attend:
                            act.wait_ge(fill, filled(i, ("SN", 1)))
                        act.activation(ws2_pair[:, :], ws2[:, r, :].bitcast(F32), ACT.Copy).then_inc(pair_done, 1)
                    elif step == "VGHI":
                        act.wait_ge(vg_in, 16 * r + 16)
                        act.wait_ge(fill, filled(i, ("VG", 7)))
                        act.activation(vg_hi[:, :, :], vg_raw[:, :, :], ACT.Copy).then_inc(vg_hi_done, 1)
                    elif step == "QKHI":
                        act.wait_ge(qk_in, 16 * r + 32)
                        act.wait_ge(fill, filled(r, ("QK", 7)))
                        act.activation(qk_hi[:, :, :], qk_raw[:, :, :], ACT.Copy).then_inc(qk_hi_done, 1)
                    elif step == "E":
                        act.wait_ge(shifted, at(i, g))
                        act.wait_ge(qe_done, at(i, g - 2))
                        act.wait_ge(totalled, at(i, g - 2))
                        act.activation(ex[:, s, :, :], okb[:, s, :, :], ACT.Exp).then_inc(exp_done, 1)
                    elif step == "T":
                        act.wait_ge(t_ready, at(i, g))
                        act.wait_ge(w_ready, at(i, g - 2))
                        act.activation(qet[:, s, :, :], bank(ps_t, 0, 256, 2), ACT.Copy).then_inc(qet_done, 1)
                    elif step == "O":
                        act.wait_ge(o_ready, at(i, g))
                        act.wait_ge(msq_done, at(i, g - 2))
                        act.wait_ge(squared, at(i, g - 1))
                        for u in range(4):
                            ins = act.activation(junk[:, u, :], ps_o[s][:, u * DK:(u + 1) * DK], ACT.Square,
                                                 accum_out=ss[:, s, u:u + 1])
                        ins.then_inc(squared, 1)
                    elif step == "OT":
                        act.wait_ge(ot_ready, at(i, g))
                        act.wait_ge(y_ready, at(i, g - 2))
                        act.activation(ogt[:, s, :, :], bank(ps_t, 0, 512, 4), ACT.Copy).then_inc(ogt_done, 1)
                    elif step == "VG":
                        if attend:
                            act.wait_ge(o_ready, at(i, n // 2))
                        act.activation(v[:, n, :], ps[:, 0:256], ACT.Copy).then_inc(v_done, 1)
                        if attend or n >= 2:
                            prev = drained(r, ("VG", n - 2)) if n >= 2 else drained(i, ("VG", n + 6))
                            act.wait_ge(drain, prev)
                        act.activation(th[:, s, :], ps[:, 256:512], ACT.Tanh, scale=0.5).then_inc(th_done, 1)
                    elif step == "ST":
                        act.wait_ge(drain, drained(r, ("ST", n)))
                        if attend:
                            act.wait_ge(w_ready, at(i, 2 * n + 1))
                        cols = slice(n * HALF, (n + 1) * HALF)
                        if not attend:
                            act.wait_ge(zeros_set, 2)
                        act.activation(es_t[0:64, 0, cols], st[0:64, n, :], ACT.Exp)
                        act.activation(es_t[64:128, 1, cols], st[64:128, n, :], ACT.Exp).then_inc(es_t_done, 1)
                    elif step == "SN":
                        act.wait_ge(drain, drained(r, ("SN", n)))
                        if attend:
                            act.wait_ge(e_ready, at(i, 2 * n + 1))
                        act.activation(es[:, 4 * n:4 * n + 4, :], sn[:, n, :].rearrange("p (b m) -> p b m", b=4),
                                       ACT.Exp).then_inc(es_done, 1)
                    elif step == "CS":
                        if attend:
                            act.wait_ge(enz_done, 2 * r + n - 1)
                        act.activation(log_cs[:, n, :], ps[:, :], ACT.Ln).then_inc(summed, 1)
                        act.wait_ge(summed, 2 * r + n + 1)
                        if attend:
                            act.wait_ge(scaled, at(i, 2 * n + 1))
                            act.wait_ge(qe_done, at(i, 2 * n + 1))
                        act.activation(enz[:, 4 * n:4 * n + 4, :], log_cs[:, n, :].rearrange("p (b m) -> p b m", b=4),
                                       ACT.Exp, scale=-1.0).then_inc(enz_done, 1)

            every_turn(act, run)

        @block.gpsimd
        def _(pool):
            for s in (qe_done, rms_done):
                pool.sem_inc(s, LEAD)
            pool.memset(minus_half[:, :], -0.5).then_inc(half_set, 1)
            pool.wait_ge(half_set, 1)
            pool.wait_ge(qk_hi_done, 1)
            pool.tensor_tensor(qk_lo[:, :, :], qk_raw[:, :, :], qk_hi[:, :, :].bitcast(F32), ALU.subtract).then_inc(qk_lo_done, 1)
            norm.pool(pool)
            pool.wait_ge(vg_hi_done, 1)
            pool.tensor_tensor(vg_lo[:, :, :], vg_raw[:, :, :], vg_hi[:, :, :].bitcast(F32), ALU.subtract).then_inc(vg_lo_done, 1)

            def run(i, attend, project, split_qk, split_vg):
                r = i + 1
                for step, n in turns(POOL_ORDER, i, attend, project, split_qk, split_vg):
                    g, s = n, n % 2
                    if step == "QK":
                        c, h, dst = n // 4, n % 4 // 2, (qt, kt)[n % 2]
                        pool.wait_ge(drain, drained(r, ("QK", n)))
                        if attend:
                            pool.wait_ge(a_ready, at(i, 2 * c + 1))
                        pool.tensor_tensor(dst[:, h, c * HALF:(c + 1) * HALF], rope_cos[:, s, :], rope_sin[:, s, :],
                                           ALU.add).then_inc(roped, 1)
                    elif step == "E":
                        pool.wait_ge(exp_done, at(i, g))
                        pool.wait_ge(enz_done, 2 * i + g // 2 + 1)
                        pool.wait_ge(t_ready, at(i, g - 2))
                        pool.tensor_tensor(qe[:, s, :, :], ex[:, s, :, :],
                                           enz[:, 2 * g:2 * g + 2, :].rearrange("p b (h m) -> p (b h) m", h=2), ALU.mult).then_inc(qe_done, 1)
                    elif step == "MS":
                        pool.wait_ge(msq_done, at(i, g))
                        pool.wait_ge(og_done, at(i, g - 2))
                        pool.tensor_tensor(rms[:, s, :], msq[:, s, :], minus_half[:, :], ALU.pow).then_inc(rms_done, 1)
                    elif step == "VGLO":
                        pool.wait_ge(vg_hi_done, r + 1)
                        pool.tensor_tensor(vg_lo[:, :, :], vg_raw[:, :, :], vg_hi[:, :, :].bitcast(F32), ALU.subtract).then_inc(vg_lo_done, 1)
                    elif step == "QKLO":
                        pool.wait_ge(qk_hi_done, r + 2)
                        pool.tensor_tensor(qk_lo[:, :, :], qk_raw[:, :, :], qk_hi[:, :, :].bitcast(F32), ALU.subtract).then_inc(qk_lo_done, 1)

            every_turn(pool, run)


XHEADS, XDIM, CTX = 32, 8, 128
STACK = 32
XV = XDIM + 1
HG = XHEADS // 4
LEAD_B = 3
TWO_PI = 2 * np.pi
TWO_PI_HI = 6.28125
ROUNDER = 1.5 * 2 ** 23

GT_KV, GT_H, GT_Q, GT_K, GT_QT, NG = 0, 1, 2, 3, 5, 7
G_ACT = {GT_H: 0, 3: 1, 5: 2, 6: 3}
G_DVE = {GT_KV: 0, GT_Q: 1, 4: 2}
X_PE = [("L2", 0), ("L2", 1), ("L1", 0), ("G", 0), ("AV", 0), ("L1", 1), ("L2", 2), ("AV", 1), ("L1", 2), ("G", 1),
    ("L1", 3), ("L2", 3), ("AV", 2), ("L2", 4), ("L1", 4), ("L2", 5), ("G", 2), ("L1", 5), ("AV", 3), ("AV", 4),
    ("AV", 5), ("L1", 6), ("L2", 6), ("L1", 7), ("L2", 7), ("G", 3), ("AV", 6), ("M", 0), ("AV", 7), ("G", 4),
    ("G", 5), ("M", 1), ("AT", 0), ("G", 6), ("OUT", 0)]
X_DVE = [("H", 0), ("L1", 0), ("L1", 1), ("L1", 2), ("G", 0), ("L1", 3), ("L1", 4), ("G", 2), ("L1", 5), ("L1", 6),
    ("L1", 7), ("NEG", 0), ("KD", 0), ("AT", 0), ("G", 4), ("M", 1), ("KD", 1), ("OUT", 0)]
X_ACT = [("L2", 0), ("L2", 1), ("L2", 2), ("V", 0), ("G", 1), ("L2", 3), ("L2", 4), ("L2", 5), ("HI", 0), ("L2", 6),
    ("L2", 7), ("G", 3), ("HI", 1), ("M", 0), ("G", 5), ("AT", 0), ("G", 6)]
X_POOL = [("CTX", 0), ("ROT", 0), ("ROT", 1), ("LO", 0), ("LO", 1), ("BIAS", 0)]
STAGE_B, STAGE_C = {"L1", "NEG", "M"}, {"L2", "AV", "AT", "OUT"}


def done(b, n=0, k=1):
    return k * (b + LEAD_B) + n + 1


def sequences(engine, run):
    run(-2, 1, "A")
    run(-1, 2, "AB")
    with engine.Fori(0, SEQS - 4, 3) as b:
        for s in range(3):
            run(b + s, s, "ABC")
    run(SEQS - 2, 0, "BC")
    run(SEQS - 1, 1, "C")


def stage_steps(order, turn, s, stages):
    for step, n in order:
        stage = "B" if step in STAGE_B else "C" if step in STAGE_C else "A"
        ahead = "CBA".index(stage)
        if stage in stages:
            yield step, n, turn + ahead, (s + ahead) % 3


def cross_attention(nc, banks, xs, con, w, a):
    ident = con[:, C_ID:C_ID + P]

    with ExitStack() as ctx:
        def sb(name, shape, dt=F32):
            return ctx.enter_context(nc.sbuf_tensor("xa_" + name, shape, dt))

        def sem(name):
            return ctx.enter_context(nc.semaphore("xa_" + name))

        wq, wkv, wout = sb("wq", [P, KC, DIM]), sb("wkv", [P, 2 * DIM]), sb("wout", [P, KC, DIM])
        bout, ctx_all, pos = sb("bout", [P, DIM]), sb("ctx_all", [P, SEQS, TOK]), sb("pos", [P, SEQS, 2])
        angle, turns_, trig = sb("angle", [P, 2, SEQS, 4]), sb("turns", [P, 2, SEQS, 4]), sb("trig", [P, 2, SEQS, 4])
        cos, sin = sb("cos", [P, SEQS, 4, 2]), sb("sin", [P, SEQS, 4, 2])
        stats, mv, var_eps = sb("stats", [P, SEQS, 6]), sb("mv", [P, SEQS, 2]), sb("var_eps", [P, SEQS])
        rstd, minus_half = sb("rstd", [P, SEQS, 1]), sb("minus_half", [P, SEQS])
        h2, h2t, ctx_b = sb("h2", [P, DIM]), sb("h2t", [P, KC, TOK]), sb("ctx_b", [P, TOK])
        by_cos, by_sin, rot = sb("by_cos", [P, 2, XHEADS, XDIM]), sb("by_sin", [P, 2, XHEADS, XDIM]), sb("rot", [P, 2, XHEADS, XDIM])
        stack = sb("stack", [P, 4, XHEADS, STACK])
        kt, qt = sb("kt", [P, 3, HG, TOK], F32R), sb("qt", [P, HG, TOK], F32R)
        k_diag, q_diag = sb("k_diag", [P, HG, 4, TOK], F32R), sb("q_diag", [P, HG, 4, TOK], F32R)
        va = sb("va", [P, 3, XHEADS, XV])
        top = sb("top", [P, HG, 4])
        wt = sb("wt", [P, 2, 4, TOK])
        rsum, att, att_t = sb("rsum", [P, XHEADS]), sb("att", [P, DIM]), sb("att_t", [P, KC, TOK])

        par_in, ctx_in, wq_in, pos_in = sem("par_in"), sem("ctx_in"), sem("wq_in"), sem("pos_in")
        wout_in, bout_in = sem("wout_in"), sem("bout_in")
        table, trig_done, tables_done, set_done = sem("table"), sem("trig_done"), sem("tables_done"), sem("set_done")
        half_set, k_diag_done = sem("half_set"), sem("k_diag_done")
        m_act, m_dve = sem("m_act"), sem("m_dve")
        stats_done, mv_done, var_done, rstd_done = sem("stats_done"), sem("mv_done"), sem("var_done"), sem("rstd_done")
        dve_sems = [sem(n) for n in ("h2_done", "neg_done", "rsum_done", "att_done", "added")]
        h2_done, neg_done, rsum_done, att_done, added = dve_sems
        g_dve, top_done = sem("g_dve"), sem("top_done")
        pe_g, pe_m, pe_l1, pe_l2, pe_av, pe_at, pe_out = [sem(n) for n in ("pe_g", "pe_m", "pe_l1", "pe_l2", "pe_av", "pe_at", "pe_out")]
        g_act, exp_done, v_done, hi_done, att_t_done = [sem(n) for n in ("g_act", "exp_done", "v_done", "hi_done", "att_t_done")]
        ctx_done, rot_done, lo_done, bias_done = [sem(n) for n in ("ctx_done", "rot_done", "lo_done", "bias_done")]

        ps_g, ps_1, ps_2, ps_av, ps_m = banks[0:2], banks[2:4], banks[4:6], banks[6], banks[7]
        block = ctx.enter_context(nc.Block())

        @block.sync
        def _(sp):
            sp.dma_start(pos[:, :, :], a["pos"].rearrange("b t p -> t b p")).then_inc(pos_in, 16)
            sp.dma_start(wkv[:, :], a["wkv"]).then_inc(par_in, 16)
            sp.dma_start(ctx_all[:, :, :], a["ctx_t"].rearrange("b c t -> c b t")).then_inc(ctx_in, 16)
            sp.dma_start(wq[:, :, :], a["xwq"]).then_inc(wq_in, 16)
            sp.dma_start(wout[:, :, :], a["wout"]).then_inc(wout_in, 16)
            sp.dma_start(bout[:, :], a["bout"].to_broadcast([P, DIM])).then_inc(bout_in, 16)
            sp.dma_start(w["w13_raw"][:, :, :, :], a["w13"]).then_inc(w["w13_in"], 16)
            sp.dma_start(w["gate_raw"][:, :, :], a["gate"]).then_inc(w["gate_in"], 16)
            sp.dma_start(w["w2"][:, :, :], a["w2"]).then_inc(w["w2_in"], 16)

        @block.tensor
        def _(pe):
            for s, k in ((pe_g, NG), (pe_m, 2), (pe_l1, 8), (pe_l2, 8), (pe_av, 8), (pe_at, 1), (pe_out, 1)):
                pe.sem_inc(s, k * LEAD_B)

            def turn_stack(ps, which, half):
                for j in range(4):
                    hg = 4 * half + j
                    mm = pe.transpose(ps[:, j * TOK:(j + 1) * TOK],
                                      stack[:, which, 4 * hg:4 * hg + 4, :].rearrange("p h c -> p (h c)"), ident)
                return mm

            def run(turn, s, stages):
                for step, n, b, p in stage_steps(X_PE, turn, s, stages):
                    if step == "G":
                        ps = ps_g[n % 2]
                        before = n - 2 if n >= 2 else (6, 5)[n]
                        last = b if n >= 2 else b - 1
                        if before in G_ACT:
                            pe.wait_ge(g_act, done(last, G_ACT[before], len(G_ACT)))
                        else:
                            pe.wait_ge(g_dve, done(last, G_DVE[before], len(G_DVE)))
                        if n == GT_KV:
                            pe.wait_ge(ctx_done, done(b))
                            if "B" not in stages:
                                pe.wait_ge(par_in, 16)
                            mm = pe.matmul(ps[:, :], ctx_b[:, :], wkv[:, :], start=True, stop=True)
                        elif n == GT_H:
                            pe.wait_ge(h2_done, done(b))
                            for kc in range(KC):
                                mm = pe.transpose(ps[:, kc * TOK:(kc + 1) * TOK], h2[:, kc * P:(kc + 1) * P], ident)
                        elif n == GT_Q:
                            pe.wait_ge(g_act, done(b, G_ACT[GT_H], len(G_ACT)))
                            if "B" not in stages:
                                pe.wait_ge(wq_in, 16)
                            for kc in range(KC):
                                mm = pe.matmul(ps[:, 0:DIM], h2t[:, kc, :], wq[:, kc, :], start=(kc == 0), stop=(kc == KC - 1))
                        else:
                            which, half = (n - GT_K) // 2, (n - GT_K) % 2
                            pe.wait_ge(lo_done, done(b, which, 2))
                            mm = turn_stack(ps, (0, 1 + p)[which], half)
                        mm.then_inc(pe_g, 1)
                    elif step == "M":
                        if n == 0:
                            pe.wait_ge(neg_done, done(b))
                        turn_stack(ps_1[n], 1 + p, n).then_inc(pe_m, 1)
                    elif step == "L1":
                        if n == 0:
                            pe.wait_ge(g_act, done(b, G_ACT[6], len(G_ACT)))
                        if n % 4 == 0:
                            pe.wait_ge(k_diag_done, done(b, n // 4, 2))
                        if n >= 2:
                            pe.wait_ge(top_done, done(b, n - 2, 8))
                        else:
                            pe.wait_ge((m_act, m_dve)[n], done(b - 1))
                        pe.matmul(ps_1[n % 2][:, :], qt[:, n, :], k_diag[:, n, :, :].rearrange("p h t -> p (h t)"),
                                  start=True, stop=True).then_inc(pe_l1, 1)
                    elif step == "L2":
                        if n % 4 == 0:
                            pe.wait_ge((m_act, m_dve)[n // 4], done(b))
                        pe.wait_ge(exp_done, done(b, n - 2, 8) if n >= 2 else done(b - 1, n + 6, 8))
                        pe.matmul(ps_2[n % 2][:, :], kt[:, p, n, :], q_diag[:, n, :, :].rearrange("p h t -> p (h t)"),
                                  start=True, stop=True).then_inc(pe_l2, 1)
                    elif step == "AV":
                        pe.wait_ge(exp_done, done(b, n, 8))
                        if n == 0:
                            pe.wait_ge(att_done, done(b - 1))
                        for j in range(4):
                            h = 4 * n + j
                            mm = pe.matmul(ps_av[:, h * XV:(h + 1) * XV], wt[:, n % 2, j, :], va[:, p, h, :], start=True, stop=True)
                        mm.then_inc(pe_av, 1)
                    elif step == "AT":
                        pe.wait_ge(att_done, done(b))
                        pe.wait_ge(added, done(b - 1))
                        for kc in range(KC):
                            mm = pe.transpose(ps_m[:, kc * TOK:(kc + 1) * TOK], att[:, kc * P:(kc + 1) * P], ident)
                        mm.then_inc(pe_at, 1)
                    elif step == "OUT":
                        pe.wait_ge(att_t_done, done(b))
                        for kc in range(KC):
                            mm = pe.matmul(ps_m[:, 0:DIM], att_t[:, kc, :], wout[:, kc, :], start=(kc == 0), stop=(kc == KC - 1))
                        mm.then_inc(pe_out, 1)

            pe.wait_ge(set_done, 5)
            pe.wait_ge(wout_in, 16)
            sequences(pe, run)

        @block.vector
        def _(dve):
            for s in dve_sems:
                dve.sem_inc(s, LEAD_B)
            dve.sem_inc(m_dve, LEAD_B)
            dve.sem_inc(k_diag_done, 2 * LEAD_B)
            dve.sem_inc(g_dve, len(G_DVE) * LEAD_B)
            dve.sem_inc(top_done, 8 * LEAD_B)
            for b in range(SEQS):
                dve.bn_stats(out=stats[:, b, :], in_=xs[:, b, :]).then_inc(stats_done, 1)
            for b in range(SEQS):
                dve.wait_ge(stats_done, b + 1)
                dve.bn_aggr(out=mv[:, b, :], in_=stats[:, b, :]).then_inc(mv_done, 1)
            dve.wait_ge(mv_done, SEQS)
            dve.tensor_scalar(var_eps[:, :], mv[:, :, 1], EPS, None, ALU.add).then_inc(var_done, 1)
            freq = con[:, C_FREQ:C_FREQ + 4].rearrange("p (a f) -> p a f", a=2)
            dve.wait_ge(pos_in, 16)
            for c in range(SEQS):
                dve.tensor_tensor(angle[:, 0, c, :].rearrange("p (a f) -> p a f", a=2), pos[:, c, :].unsqueeze(2).to_broadcast([P, 2, 2]),
                                  freq, ALU.mult).then_inc(table, 1)
            n = SEQS
            dve.wait_ge(table, n)
            dve.tensor_scalar(angle[:, 1, :, :], angle[:, 0, :, :], np.pi / 2, None, ALU.add).then_inc(table, 1)
            dve.wait_ge(table, n + 1)
            dve.tensor_scalar(turns_[:, :, :, :], angle[:, :, :, :], 1 / TWO_PI, ROUNDER, ALU.mult, ALU.add).then_inc(table, 1)
            dve.wait_ge(table, n + 2)
            dve.tensor_scalar(turns_[:, :, :, :], turns_[:, :, :, :], ROUNDER, None, ALU.subtract).then_inc(table, 1)
            dve.wait_ge(table, n + 3)
            dve.scalar_tensor_tensor(out=angle[:, :, :, :], in0=turns_[:, :, :, :], scalar=-TWO_PI_HI, in1=angle[:, :, :, :],
                                     op0=ALU.mult, op1=ALU.add).then_inc(table, 1)
            dve.wait_ge(table, n + 4)
            dve.scalar_tensor_tensor(out=angle[:, :, :, :], in0=turns_[:, :, :, :], scalar=-(TWO_PI - TWO_PI_HI), in1=angle[:, :, :, :],
                                     op0=ALU.mult, op1=ALU.add).then_inc(table, 1)
            dve.wait_ge(table, n + 5)
            dve.tensor_scalar(angle[:, :, :, :], angle[:, :, :, :], -3.1415925, 3.1415925, ALU.max, ALU.min).then_inc(table, 1)
            dve.wait_ge(trig_done, 1)
            for c in range(2):
                dve.tensor_copy(cos[:, :, :, c], trig[:, 1, :, :]).then_inc(tables_done, 1)
                dve.tensor_scalar(sin[:, :, :, c], trig[:, 0, :, :], 2.0 * c - 1.0, None, ALU.mult).then_inc(tables_done, 1)
            dve.wait_ge(tables_done, 4)
            dve.wait_ge(rstd_done, 1)
            dve.wait_ge(set_done, 5)

            def run(turn, s, stages):
                for step, n, b, p in stage_steps(X_DVE, turn, s, stages):
                    if step == "H":
                        dve.wait_ge(pe_g, done(b - 1, GT_H, NG))
                        dve.tensor_scalar(h2[:, :], xs[:, b, :], mv[:, b, 0:1], rstd[:, b, 0:1], ALU.subtract, ALU.mult).then_inc(h2_done, 1)
                    elif step == "G" and n == 4:
                        dve.wait_ge(pe_g, done(b, n, NG))
                        dve.wait_ge(pe_l2, done(b - 3, 7, 8))
                        dve.tensor_copy(kt[:, p, 4:8, :], bank(ps_g[0], 0, 512, 4)).then_inc(g_dve, 1)
                    elif step == "KD":
                        if n == 0:
                            dve.wait_ge(g_act, done(b, G_ACT[3], len(G_ACT)))
                        else:
                            dve.wait_ge(g_dve, done(b, G_DVE[4], len(G_DVE)))
                        dve.wait_ge(pe_l1, done(b - 1, 4 * n + 3, 8))
                        groups = slice(4 * n, 4 * n + 4)
                        for hl in range(4):
                            part = slice(hl * QUAD, hl * QUAD + 3 * XDIM)
                            ins = dve.tensor_copy(k_diag[part, groups, hl, :], kt[part, p, groups, :])
                        ins.then_inc(k_diag_done, 1)
                    elif step == "M":
                        dve.wait_ge(pe_m, done(b, 1, 2))
                        dve.wait_ge(pe_l2, done(b - 1, 7, 8))
                        for hl in range(4):
                            part = slice(hl * QUAD, hl * QUAD + 3 * XDIM + 1)
                            ins = dve.tensor_copy(q_diag[part, 4:8, hl, :], bank(ps_1[1], 0, 512, 4)[part])
                        ins.then_inc(m_dve, 1)
                    elif step == "G":
                        which = G_DVE[n]
                        ps = ps_g[n % 2][:, 0:DIM].rearrange("p (h c) -> p h c", c=XDIM)
                        dve.wait_ge(pe_g, done(b, n, NG))
                        if n == GT_KV:
                            dve.wait_ge(v_done, done(b))
                        dve.wait_ge(rot_done, done(b - 1, which, 2))
                        cos_b = cos[:, b, :, :].rearrange("p f c -> p (f c)").unsqueeze(1).to_broadcast([P, XHEADS, XDIM])
                        pairs = ps.rearrange("p h (f c) -> p h f c", c=2)
                        out2 = by_sin[:, which, :, :].rearrange("p h (f c) -> p h f c", c=2)
                        dve.tensor_tensor(by_cos[:, which, :, :], ps, cos_b, ALU.mult)
                        for c in range(2):
                            sin_b = sin[:, b, :, c].unsqueeze(1).to_broadcast([P, XHEADS, 4])
                            ins = dve.tensor_tensor(out2[:, :, :, c], pairs[:, :, :, 1 - c], sin_b, ALU.mult)
                        ins.then_inc(g_dve, 1)
                    elif step == "L1":
                        dve.wait_ge(pe_l1, done(b, n, 8))
                        dve.tensor_reduce(top[:, n, :], bank(ps_1[n % 2], 0, 512, 4), AX.X, ALU.max).then_inc(top_done, 1)
                    elif step == "NEG":
                        dve.wait_ge(top_done, done(b, 7, 8))
                        dve.tensor_scalar(stack[:, 1 + p, :, 3 * XDIM].bitcast(F32R), top[:, :, :].rearrange("p g h -> p (g h)"), -1.0, None,
                                          ALU.mult).then_inc(neg_done, 1)
                    elif step == "AT":
                        av = ps_av[:, 0:XHEADS * XV].rearrange("p (h c) -> p h c", c=XV)
                        dve.wait_ge(pe_av, done(b, 7, 8))
                        dve.reciprocal(rsum[:, :], av[:, :, XDIM]).then_inc(rsum_done, 1)
                        dve.wait_ge(rsum_done, done(b))
                        dve.wait_ge(pe_at, done(b - 1))
                        dve.tensor_tensor(att[:, :].rearrange("p (h c) -> p h c", c=XDIM), av[:, :, 0:XDIM],
                                          rsum[:, :].unsqueeze(2).to_broadcast([P, XHEADS, XDIM]), ALU.mult).then_inc(att_done, 1)
                    elif step == "OUT":
                        dve.wait_ge(pe_out, done(b))
                        dve.wait_ge(bias_done, done(b))
                        dve.tensor_tensor(xs[:, b, :], ps_m[:, 0:DIM], xs[:, b, :], ALU.add).then_inc(added, 1)

            sequences(dve, run)

        @block.scalar
        def _(act):
            act.sem_inc(g_act, len(G_ACT) * LEAD_B)
            act.sem_inc(exp_done, 8 * LEAD_B)
            act.sem_inc(v_done, LEAD_B)
            act.sem_inc(hi_done, 2 * LEAD_B)
            act.sem_inc(att_t_done, LEAD_B)
            act.sem_inc(m_act, LEAD_B)
            act.wait_ge(table, SEQS + 6)
            act.activation(trig[:, :, :, :], angle[:, :, :, :], ACT.Sin).then_inc(trig_done, 1)

            def run(turn, s, stages):
                for step, n, b, p in stage_steps(X_ACT, turn, s, stages):
                    if step == "L2":
                        act.wait_ge(pe_l2, done(b, n, 8))
                        act.wait_ge(pe_av, done(b, n - 2, 8) if n >= 2 else done(b - 1, n + 6, 8))
                        act.activation(wt[:, n % 2, :, :], bank(ps_2[n % 2], 0, 512, 4), ACT.Exp, scale=XDIM ** -0.5).then_inc(exp_done, 1)
                    elif step == "V":
                        act.wait_ge(pe_g, done(b, GT_KV, NG))
                        act.wait_ge(pe_av, done(b - 3, 7, 8))
                        act.activation(va[:, p, :, 0:XDIM], ps_g[0][:, DIM:2 * DIM].rearrange("p (h c) -> p h c", c=XDIM),
                                       ACT.Copy).then_inc(v_done, 1)
                    elif step == "G" and n == GT_H:
                        act.wait_ge(pe_g, done(b, n, NG))
                        act.wait_ge(pe_g, done(b - 1, GT_Q, NG))
                        act.activation(h2t[:, :, :], bank(ps_g[1], 0, DIM, KC), ACT.Copy).then_inc(g_act, 1)
                    elif step == "G":
                        act.wait_ge(pe_g, done(b, n, NG))
                        ps = bank(ps_g[n % 2], 0, 512, 4)
                        if n == 3:
                            act.wait_ge(pe_l2, done(b - 3, 7, 8))
                            ins = act.activation(kt[:, p, 0:4, :], ps, ACT.Copy)
                        else:
                            act.wait_ge(pe_l1, done(b - 1, 7, 8))
                            ins = act.activation(qt[:, 4 * (n - 5):4 * (n - 4), :], ps, ACT.Copy)
                        ins.then_inc(g_act, 1)
                    elif step == "M":
                        act.wait_ge(pe_m, done(b, 0, 2))
                        act.wait_ge(pe_l2, done(b - 1, 7, 8))
                        for hl in range(4):
                            part = slice(hl * QUAD, hl * QUAD + 3 * XDIM + 1)
                            ins = act.activation(q_diag[part, 0:4, hl, :], bank(ps_1[0], 0, 512, 4)[part], ACT.Copy)
                        ins.then_inc(m_act, 1)
                    elif step == "HI":
                        act.wait_ge(rot_done, done(b, n, 2))
                        if n == 0:
                            act.wait_ge(pe_g, done(b - 1, 4, NG))
                        else:
                            act.wait_ge(pe_m, done(b - 3, 1, 2))
                        for at_ in ((0, 1), (0, 2))[n]:
                            ins = act.activation(stack[:, (0, 1 + p)[n], :, at_ * XDIM:(at_ + 1) * XDIM].bitcast(F32R), rot[:, n, :, :], ACT.Copy)
                        ins.then_inc(hi_done, 1)
                    elif step == "AT":
                        act.wait_ge(pe_at, done(b))
                        act.wait_ge(pe_out, done(b - 1))
                        act.activation(att_t[:, :, :], bank(ps_m, 0, DIM, KC), ACT.Copy).then_inc(att_t_done, 1)

            act.wait_ge(set_done, 5)
            act.preload_act_table_set("natural_log_exp_and_others")
            sequences(act, run)

        @block.gpsimd
        def _(pool):
            for s, k in ((ctx_done, 1), (rot_done, 2), (lo_done, 2), (bias_done, 1)):
                pool.sem_inc(s, k * LEAD_B)
            pool.memset(minus_half[:, :], -0.5).then_inc(half_set, 1)
            pool.wait_ge(half_set, 1)
            pool.wait_ge(var_done, 1)
            pool.tensor_tensor(rstd[:, :, 0], var_eps[:, :], minus_half[:, :], ALU.pow).then_inc(rstd_done, 1)
            pool.memset(va[:, :, :, :], 1.0).then_inc(set_done, 1)
            pool.memset(stack[:, 1:4, :, 3 * XDIM:], 0.0).then_inc(set_done, 1)
            pool.memset(stack[:, 0, :, 3 * XDIM:], 1.0).then_inc(set_done, 1)
            pool.memset(k_diag[:, :, :, :].bitcast(F32), 0.0).then_inc(set_done, 1)
            pool.memset(q_diag[:, :, :, :].bitcast(F32), 0.0).then_inc(set_done, 1)
            pool.wait_ge(ctx_in, 16)
            pool.wait_ge(bout_in, 16)

            def run(turn, s, stages):
                for step, n, b, p in stage_steps(X_POOL, turn, s, stages):
                    if step == "CTX":
                        pool.wait_ge(pe_g, done(b - 1, GT_KV, NG))
                        pool.tensor_copy(ctx_b[:, :], ctx_all[:, b, :]).then_inc(ctx_done, 1)
                    elif step == "ROT":
                        pool.wait_ge(g_dve, done(b, n, len(G_DVE)))
                        pool.wait_ge(lo_done, done(b - 1, n, 2))
                        pool.tensor_tensor(rot[:, n, :, :], by_cos[:, n, :, :], by_sin[:, n, :, :], ALU.add).then_inc(rot_done, 1)
                    elif step == "LO":
                        pool.wait_ge(hi_done, done(b, n, 2))
                        lo = (2, 1)[n]
                        which = (0, 1 + p)[n]
                        pool.tensor_tensor(stack[:, which, :, lo * XDIM:(lo + 1) * XDIM].bitcast(F32R), rot[:, n, :, :],
                                           stack[:, which, :, 0:XDIM], ALU.subtract).then_inc(lo_done, 1)
                    elif step == "BIAS":
                        pool.wait_ge(h2_done, done(b))
                        pool.tensor_tensor(xs[:, b, :], xs[:, b, :], bout[:, :], ALU.add).then_inc(bias_done, 1)

            sequences(pool, run)


EXPERTS, HID, TOPK = 8, 128, 2
NE = EXPERTS + 1


def feed_forward(nc, banks, xs, hn, ht_hi, ht_lo, con, w, a, out):
    ident = con[:, C_ID:C_ID + P]

    with ExitStack() as ctx:
        def sb(name, shape, dt=F32):
            return ctx.enter_context(nc.sbuf_tensor("ff_" + name, shape, dt))

        def sem(name):
            return ctx.enter_context(nc.semaphore("ff_" + name))

        one_plus, score = sb("one_plus", [P, SEQS, EXPERTS]), sb("score", [P, SEQS, EXPERTS])
        above, same = sb("above", [P, SEQS, EXPERTS, EXPERTS]), sb("same", [P, SEQS, EXPERTS, EXPERTS])
        rank, scale = sb("rank", [P, SEQS, EXPERTS]), sb("scale", [P, NE, SEQS])
        act_out, hid, hid_t = sb("act_out", [P, 2, HID]), sb("hid", [P, 2, HID]), sb("hid_t", [P, 2, TOK])

        norm = Norm(nc, ctx, banks, xs, hn, ht_hi, ht_lo, ident, "norm3")
        ones_set, routed, exp_done, step_done, scale_done = [sem(n) for n in ("ones_set", "routed", "exp_done", "step_done", "scale_done")]
        up, silu_done, hid_done, turned, hid_t_done, down, added, stored = [
            sem(n) for n in ("up", "silu_done", "hid_done", "turned", "hid_t_done", "down", "added", "stored")]
        w_hi_done, w_lo_done, gate_hi_done, gate_lo_done = [sem(n) for n in ("w_hi_done", "w_lo_done", "gate_hi_done", "gate_lo_done")]

        ps_u, ps_t, ps_y, ps_r = banks[0:2], banks[2:4], banks[4:8], banks[2]
        block = ctx.enter_context(nc.Block())

        def tile(t, b):
            return SEQS * t + b + 1

        @block.sync
        def _(sp):
            for c in range(4):
                sp.wait_ge(added, c + 1)
                sp.dma_start(out[2 * c:2 * c + 2].rearrange("b t d -> t b d"), xs[:, 2 * c:2 * c + 2, :]).then_inc(stored, 16)
            sp.wait_ge(stored, 4 * 16)

        @block.tensor
        def _(pe):
            norm.tensor(pe)
            pe.wait_ge(norm.lo_done, 4)
            pe.wait_ge(gate_lo_done, 1)
            for b in range(SEQS):
                cols = slice(b * TOK, (b + 1) * TOK)
                for kc in range(KC):
                    mm = split_product(pe, ps_r[:, b * EXPERTS:(b + 1) * EXPERTS], ht_hi[:, kc, cols], ht_lo[:, kc, cols],
                                       w["gate_hi"][:, kc, :], w["gate_lo"][:, kc, :], kc == 0, kc == KC - 1)
            mm.then_inc(routed, 1)
            pe.wait_ge(w_lo_done, NE)
            pe.wait_ge(w["w2_in"], 16)

            def turn_over(t, b):
                pe.wait_ge(hid_done, tile(t, b))
                if not (isinstance(t, int) and t == 0 and b < 2):
                    pe.wait_ge(hid_t_done, tile(t, b - 2))
                else:
                    pe.wait_ge(exp_done, 1)
                pe.transpose(ps_t[b % 2][:, 0:TOK], hid[:, b % 2, :], ident).then_inc(turned, 1)

            def project(t, b):
                pe.wait_ge(hid_t_done, tile(t, b))
                pe.matmul(ps_y[b // 2][:, b % 2 * DIM:(b % 2 + 1) * DIM], hid_t[:, b % 2, :], w["w2"][:, t, :],
                          start=isinstance(t, int) and t == 0 and b % 2 == 0, stop=False, skip_group_check=True).then_inc(down, 1)

            def run(t, first):
                for b in range(SEQS):
                    if not first or b >= 2:
                        pe.wait_ge(hid_done, tile(t, b - 2))
                    for kc in range(KC):
                        mm = split_product(pe, ps_u[b % 2][:, 0:2 * HID], ht_hi[:, kc, b * TOK:(b + 1) * TOK],
                                           ht_lo[:, kc, b * TOK:(b + 1) * TOK], w["w13_hi"][:, kc, t, :], w["w13_lo"][:, kc, t, :],
                                           kc == 0, kc == KC - 1)
                    mm.then_inc(up, 1)
                    if b >= 2:
                        turn_over(t, b - 2)
                    elif not first:
                        turn_over(t - 1, b + 6)
                    if b >= 4:
                        project(t, b - 4)
                    elif not first:
                        project(t - 1, b + 4)

            run(0, True)
            run(1, False)
            with pe.Fori(2, NE) as t:
                run(t, False)
            turn_over(NE - 1, 6)
            project(NE - 1, 4)
            turn_over(NE - 1, 7)
            for b in (5, 6, 7):
                project(NE - 1, b)

        @block.vector
        def _(dve):
            norm.vector_norm(dve)
            dve.memset(scale[:, 0, :], 1.0).then_inc(ones_set, 1)
            dve.wait_ge(gate_hi_done, 1)
            dve.tensor_tensor(w["gate_lo"][:, :, :], w["gate_raw"][:, :, :], w["gate_hi"][:, :, :].bitcast(F32), ALU.subtract).then_inc(gate_lo_done, 1)
            norm.vector_low(dve)
            for e in range(NE):
                dve.wait_ge(w_hi_done, e + 1)
                dve.tensor_tensor(w["w13_lo"][:, :, e, :], w["w13_raw"][:, :, e, :], w["w13_hi"][:, :, e, :].bitcast(F32), ALU.subtract).then_inc(w_lo_done, 1)

            def hidden(t, b):
                dve.wait_ge(silu_done, tile(t, b))
                if not (isinstance(t, int) and t == 0 and b < 2):
                    dve.wait_ge(turned, tile(t, b - 2))
                dve.scalar_tensor_tensor(out=hid[:, b % 2, :], in0=ps_u[b % 2][:, HID:2 * HID], scalar=scale[:, t, b:b + 1],
                                         in1=act_out[:, b % 2, :], op0=ALU.mult, op1=ALU.mult).then_inc(hid_done, 1)

            def link(ins, n):
                ins.then_inc(step_done, 1)
                dve.wait_ge(step_done, n)

            dve.wait_ge(exp_done, 1)
            link(dve.tensor_scalar(one_plus[:, :, :], one_plus[:, :, :], 1.0, None, ALU.add), 1)
            link(dve.reciprocal(score[:, :, :], one_plus[:, :, :]), 2)
            before = con[:, C_BEFORE:C_BEFORE + 64]
            for b in range(SEQS):
                own = score[:, b, :].unsqueeze(2).to_broadcast([P, EXPERTS, EXPERTS])
                other = score[:, b, :].unsqueeze(1).to_broadcast([P, EXPERTS, EXPERTS])
                dve.tensor_tensor(above[:, b, :, :], other, own, ALU.is_gt)
                ins = dve.tensor_tensor(same[:, b, :, :], other, own, ALU.is_equal)
            link(ins, 3)
            link(dve.tensor_tensor(same[:, :, :, :].rearrange("p b e f -> p b (e f)"), same[:, :, :, :].rearrange("p b e f -> p b (e f)"),
                                   before.unsqueeze(1).to_broadcast([P, SEQS, 64]), ALU.mult), 4)
            link(dve.tensor_tensor(above[:, :, :, :], above[:, :, :, :], same[:, :, :, :], ALU.add), 5)
            link(dve.tensor_reduce(rank[:, :, :], above[:, :, :, :], AX.X, ALU.add), 6)
            link(dve.tensor_scalar(rank[:, :, :], rank[:, :, :], TOPK - 0.5, None, ALU.is_lt), 7)
            dve.tensor_tensor(scale[:, 1:NE, :].rearrange("p e b -> p b e"), rank[:, :, :], score[:, :, :], ALU.mult).then_inc(scale_done, 1)
            dve.wait_ge(scale_done, 1)

            for t in range(2):
                for b in range(SEQS):
                    hidden(t, b)
            with dve.Fori(2, NE) as t:
                for b in range(SEQS):
                    hidden(t, b)
            for c in range(4):
                dve.wait_ge(down, tile(NE - 1, 2 * c + 1))
                dve.tensor_tensor(xs[:, 2 * c:2 * c + 2, :], bank(ps_y[c], 0, 512, 2), xs[:, 2 * c:2 * c + 2, :], ALU.add).then_inc(added, 1)

        @block.scalar
        def _(act):
            act.wait_ge(w["gate_in"], 16)
            act.wait_ge(w["w13_in"], 16)
            act.activation(w["gate_hi"][:, :, :], w["gate_raw"][:, :, :], ACT.Copy).then_inc(gate_hi_done, 1)
            for e in range(NE):
                act.activation(w["w13_hi"][:, :, e, :], w["w13_raw"][:, :, e, :], ACT.Copy).then_inc(w_hi_done, 1)
            norm.scalar(act)
            act.wait_ge(routed, 1)
            act.activation(one_plus[:, :, :], ps_r[:, 0:SEQS * EXPERTS].rearrange("p (b e) -> p b e", b=SEQS), ACT.Exp,
                           scale=-1.0).then_inc(exp_done, 1)

            def silu(t, b):
                act.wait_ge(up, tile(t, b))
                if not (isinstance(t, int) and t == 0 and b < 2):
                    act.wait_ge(hid_done, tile(t, b - 2))
                act.activation(act_out[:, b % 2, :], ps_u[b % 2][:, 0:HID], ACT.Silu, scale=scale[:, t, b:b + 1]).then_inc(silu_done, 1)

            def keep(t, b):
                act.wait_ge(turned, tile(t, b))
                if not (isinstance(t, int) and t == 0 and b < 2):
                    act.wait_ge(down, tile(t, b - 2))
                act.activation(hid_t[:, b % 2, :], ps_t[b % 2][:, 0:TOK], ACT.Copy).then_inc(hid_t_done, 1)

            def run(t, first):
                for b in range(SEQS):
                    silu(t, b)
                    if b >= 2:
                        keep(t, b - 2)
                    elif not first:
                        keep(t - 1, b + 6)

            act.wait_ge(ones_set, 1)
            run(0, True)
            act.wait_ge(scale_done, 1)
            run(1, False)
            with act.Fori(2, NE) as t:
                run(t, False)
            keep(NE - 1, 6)
            keep(NE - 1, 7)

        @block.gpsimd
        def _(pool):
            norm.pool(pool)


def decoder_layer(nc, a, out):
    with ExitStack() as ctx:
        def sb(name, shape, dt=F32):
            return ctx.enter_context(nc.sbuf_tensor(name, shape, dt))

        banks = [ctx.enter_context(nc.psum_tensor(f"bank{n}", [P, 512], F32)) for n in range(8)]
        xs = sb("xs", [P, SEQS, DIM])
        hn = sb("hn", [P, SEQS, DIM])
        ht_hi, ht_lo = sb("ht_hi", [P, KC, ALL], F32R), sb("ht_lo", [P, KC, ALL], F32R)
        con = sb("con", [P, C_ALL])
        x_in = [ctx.enter_context(nc.semaphore(f"x_in{n}")) for n in range(2)]
        slot_attention(nc, banks, xs, hn, ht_hi, ht_lo, con, x_in, a)

        w = dict(
            w13_raw=sb("w13_raw", [P, KC, NE, 2 * HID]), w13_hi=sb("w13_hi", [P, KC, NE, 2 * HID], F32R),
            w13_lo=sb("w13_lo", [P, KC, NE, 2 * HID], F32R), w2=sb("w2", [P, NE, DIM]),
            gate_raw=sb("gate_raw", [P, KC, EXPERTS]), gate_hi=sb("gate_hi", [P, KC, EXPERTS], F32R),
            gate_lo=sb("gate_lo", [P, KC, EXPERTS], F32R),
            w13_in=ctx.enter_context(nc.semaphore("w13_in")), gate_in=ctx.enter_context(nc.semaphore("gate_in")),
            w2_in=ctx.enter_context(nc.semaphore("w2_in")))
        cross_attention(nc, banks, xs, con, w, a)
        feed_forward(nc, banks, xs, hn, ht_hi, ht_lo, con, w, a, out)


def layouts(i):
    def rows(m):
        return m.reshape(KC, P, -1).transpose(1, 0, 2)

    def heads(m):
        return rows(m).reshape(P, KC, PAIRS, 2, DK).transpose(2, 0, 1, 3, 4)

    q, k, v, g = (heads(i["L0_attn_" + n].T) for n in ("Wq", "Wk", "Wv", "Wg"))
    ws1 = np.zeros((P, KC, P), np.float32)
    ws2 = np.zeros((P, PAIRS, P), np.float32)
    for n in range(4):
        ws1[:, :, QUAD * n:QUAD * n + S_RANK] = rows(i["L0_attn_Ws1"].T)
        ws2[QUAD * n:QUAD * n + S_RANK] = i["L0_attn_Ws2"].T.reshape(S_RANK, PAIRS, P)
        ws2[QUAD * n + S_RANK] = i["L0_attn_bs2"].reshape(PAIRS, P)
    w1 = np.concatenate([i["L0_ffn_sw1"][None], i["L0_ffn_w1"]])
    w3 = np.concatenate([i["L0_ffn_sw3"][None], i["L0_ffn_w3"]])
    w2 = np.concatenate([i["L0_ffn_sw2"][None], i["L0_ffn_w2"]])
    return {
        "x": i["x"],
        "constants": constants(),
        "wqk": np.stack([q, k], axis=4).reshape(PAIRS, P, KC, 512),
        "wvg": np.stack([v, g], axis=3).reshape(PAIRS, P, KC, 512),
        "ws1": ws1,
        "ws2": ws2,
        "g_norm": i["L0_attn_g_norm_weight"].reshape(P, 1),
        "wo": i["L0_attn_Wo"].T.reshape(HEADS, P, DIM).transpose(1, 0, 2),
        "pos": i["fside_BxSx2_0"],
        "ctx_t": i["ctx_1024"].transpose(0, 2, 1),
        "xwq": rows(i["L0_xattn_Wq"]),
        "wkv": i["L0_xattn_Wkv"],
        "wout": rows(i["L0_xattn_Wout"]),
        "bout": i["L0_xattn_bout"].reshape(1, DIM),
        "gate": rows(i["L0_ffn_gate_w"].T),
        "w13": np.stack([w1, w3], axis=1).reshape(NE * 2 * HID, DIM).T.reshape(KC, P, NE, 2 * HID).transpose(1, 0, 2, 3),
        "w2": w2.transpose(2, 0, 1),
    }


def kernel(**inputs):
    import numpy as _np
    import concourse.bacc as _bacc
    from concourse import mybir as _mybir
    from concourse.bass_utils import run_bass_kernel_spmd as _run

    nc = _bacc.Bacc("TRN2", target_bir_lowering=False, num_devices=1)
    arrays = {n: _np.ascontiguousarray(m) for n, m in layouts({n: _np.asarray(m) for n, m in inputs.items()}).items()}
    handles = {n: nc.dram_tensor(f"in_{n}", m.shape, _mybir.dt.from_np(m.dtype), kind="ExternalInput").ap() for n, m in arrays.items()}
    out = nc.dram_tensor("out", (SEQS, TOK, DIM), F32, kind="ExternalOutput").ap()
    decoder_layer(nc, handles, out)
    r = _run(nc, [{f"in_{n}": m for n, m in arrays.items()}], core_ids=[0])
    return r.results[0]["out"]
```

```python
from contextlib import ExitStack

import numpy as np

import concourse.bass as bass
from concourse import mybir

F32 = mybir.dt.float32
F32R = mybir.dt.float32r
ALU = mybir.AluOpType
ACT = mybir.ActivationFunctionType
AX = mybir.AxisListType

P = 128
SEQS, TOK, DIM = 8, 128, 256
KC = DIM // P
ALL = SEQS * TOK
HALF = ALL // 2
EPS = 1e-5

HEADS, DK, SLOTS = 16, 128, 64
PAIRS = HEADS // 2
GROUPS = SEQS // 2
CLAMP = 32.0
S_RANK = 16
QUAD = 32

C_TRI, C_TRIS, C_ID, C_COS, C_SIN, C_ONE, C_FREQ, C_BEFORE, C_LOW_W, C_LOW_U = 0, 128, 256, 384, 512, 640, 641, 645, 709, 710
C_ALL = C_LOW_U + 1


def constants():
    c = np.zeros((P, C_ALL), np.float32)
    j, t = np.arange(P)[:, None], np.arange(TOK)[None, :]
    c[:, C_TRI:C_TRI + TOK] = j <= t
    c[:, C_TRIS:C_TRIS + TOK] = (j <= t) * np.float32(DK ** -0.5)
    c[:, C_ID:C_ID + P] = np.eye(P)
    freq = (1.0 / 10000.0 ** (np.arange(0, DK, 2, dtype=np.float32) / np.float32(DK))).astype(np.float32)
    angle = (np.arange(TOK, dtype=np.float32)[None, :] * freq[:, None]).astype(np.float32)
    cos, sin = np.cos(angle.astype(np.float64)), np.sin(angle.astype(np.float64))
    c[:, C_COS:C_COS + TOK] = np.concatenate([cos, cos])
    c[:, C_SIN:C_SIN + TOK] = np.concatenate([sin, -sin])
    c[[S_RANK, QUAD + S_RANK], C_ONE] = 1.0
    c[:, C_FREQ:C_FREQ + 4] = [1.0, 10000.0 ** -0.5, 1.0, 10000.0 ** -0.5]
    c[QUAD:2 * QUAD, C_LOW_W] = c[3 * QUAD:, C_LOW_W] = -1.0
    c[2 * QUAD:, C_LOW_U] = -1.0
    e = np.arange(8)
    c[:, C_BEFORE:C_BEFORE + 64] = (e[None, :] < e[:, None]).astype(np.float32).reshape(1, 64)
    return c


FILLS = [("QK", 0), ("ST", 0), ("QK", 1), ("SN", 0), ("QK", 2), ("VG", 0), ("VG", 1), ("QK", 3), ("QK", 4),
    ("SN", 1), ("VG", 2), ("QK", 5), ("QK", 6), ("VG", 3), ("ST", 1), ("VG", 4), ("VG", 5), ("QK", 7), ("VG", 6),
    ("VG", 7), ("CS", 0), ("CS", 1)]
NFILL = len(FILLS)
NDRAIN = NFILL - 2
PLACE = {f: n for n, f in enumerate(FILLS)}
SPREAD = 14
LEAD = 4


def at(i, g):
    return 4 * i + g + 1 + LEAD


def fill_bank(place, attend):
    return place % 8 if place < SPREAD and not attend else place % 2


def last_use(place):
    same = [p for p in range(place) if fill_bank(p, False) == fill_bank(place, False)]
    return max(same, default=None)


def filled(r, f):
    return NFILL * r + PLACE[f] + 1


def drained(r, f):
    return NDRAIN * r + PLACE[f] + 1


PE_ORDER = [("A", 0), ("E", 0), ("A", 1), ("QK", 0), ("ST", 0), ("E", 1), ("T", 0), ("A", 2), ("W", 0), ("QK", 1),
    ("O", 0), ("E", 2), ("SN", 0), ("A", 3), ("QK", 2), ("T", 1), ("VG", 0), ("E", 3), ("W", 1), ("VG", 1), ("T", 2),
    ("QK", 3), ("O", 1), ("W", 2), ("T", 3), ("QK", 4), ("SN", 1), ("OT", 0), ("O", 2), ("W", 3), ("VG", 2),
    ("QK", 5), ("Y", 0), ("QK", 6), ("VG", 3), ("OT", 1), ("O", 3), ("ST", 1), ("VG", 4), ("VG", 5), ("Y", 1),
    ("OT", 2), ("QK", 7), ("VG", 6), ("OT", 3), ("Y", 2), ("VG", 7), ("Y", 3), ("CS", 0), ("CS", 1)]
DVE_ORDER = [("A", 0), ("E", 0), ("A", 1), ("SUM", 0), ("QK", 0), ("E", 1), ("W", 0), ("A", 2), ("ST", 0), ("QK", 1),
    ("SN", 0), ("A", 3), ("MS", 0), ("E", 2), ("QK", 2), ("O", 0), ("SUM", 1), ("VG", 0), ("W", 1), ("E", 3),
    ("VG", 1), ("QK", 3), ("SUM", 2), ("W", 2), ("MS", 1), ("QK", 4), ("OT", 0), ("SN", 1), ("MS", 2), ("O", 1),
    ("VG", 2), ("QK", 5), ("W", 3), ("QK", 6), ("VG", 3), ("OT", 1), ("ST", 1), ("Y", 0), ("O", 2), ("SUM", 3),
    ("MS", 3), ("VG", 4), ("VG", 5), ("Y", 1), ("O", 3), ("OT", 2), ("QK", 7), ("OT", 3), ("VG", 6), ("Y", 2),
    ("VG", 7), ("Y", 3)]
ACT_ORDER = [("W2P", 0), ("E", 0), ("T", 0), ("VGHI", 0), ("E", 1), ("O", 0), ("E", 2), ("T", 1), ("VG", 0),
    ("SN", 0), ("VG", 1), ("WOHI", 0), ("T", 2), ("E", 3), ("ST", 0), ("O", 1), ("T", 3), ("OT", 0), ("O", 2),
    ("VG", 2), ("SN", 1), ("VG", 3), ("OT", 1), ("O", 3), ("VG", 4), ("VG", 5), ("OT", 2), ("VG", 6), ("OT", 3),
    ("QKHI", 0), ("ST", 1), ("VG", 7), ("CS", 0), ("CS", 1)]
POOL_ORDER = [("E", 0), ("WO", 0), ("QK", 0), ("VGLO", 0), ("E", 1), ("QK", 1), ("MS", 0), ("E", 2), ("QK", 2),
    ("E", 3), ("WOLO", 0), ("QK", 3), ("SN", 0), ("MS", 1), ("QK", 4), ("MS", 2), ("QK", 5), ("QK", 6), ("MS", 3),
    ("QK", 7), ("SN", 1), ("QKLO", 0)]
PE_LAST = [("A", 0), ("A", 1), ("E", 0), ("A", 2), ("E", 1), ("T", 0), ("A", 3), ("W", 0), ("E", 2), ("T", 1),
    ("O", 0), ("W", 1), ("E", 3), ("O", 1), ("T", 2), ("W", 2), ("T", 3), ("OT", 0), ("O", 2), ("W", 3), ("OT", 1),
    ("Y", 0), ("O", 3), ("Y", 1), ("OT", 2), ("Y", 2), ("OT", 3), ("Y", 3)]
DVE_LAST = [("A", 0), ("A", 1), ("E", 0), ("A", 2), ("SUM", 0), ("E", 1), ("A", 3), ("W", 0), ("SUM", 1), ("E", 2),
    ("W", 1), ("MS", 0), ("E", 3), ("SUM", 2), ("O", 0), ("MS", 1), ("W", 2), ("SUM", 3), ("O", 1), ("OT", 0),
    ("MS", 2), ("W", 3), ("OT", 1), ("Y", 0), ("O", 2), ("N2", 0), ("MS", 3), ("Y", 1), ("OT", 2), ("O", 3),
    ("N2", 1), ("Y", 2), ("OT", 3), ("N2", 2), ("Y", 3), ("N2", 3)]
ACT_LAST = [("WOHI", 0), ("E", 0), ("T", 0), ("E", 1), ("T", 1), ("O", 0), ("E", 2), ("T", 2), ("E", 3), ("O", 1),
    ("T", 3), ("OT", 0), ("O", 2), ("OT", 1), ("O", 3), ("OT", 2), ("OT", 3)]
POOL_LAST = [("WO", 0), ("WOLO", 0), ("E", 0), ("E", 1), ("E", 2), ("MS", 0), ("E", 3), ("MS", 1), ("MS", 2),
    ("MS", 3), ("N2", 0), ("N2", 1), ("N2", 2), ("N2", 3)]
DVE_FIRST = [("QK", 0), ("ST", 0), ("QK", 1), ("SN", 0), ("QK", 2), ("VG", 0), ("VG", 1), ("QK", 3), ("QK", 4),
    ("SN", 1), ("VG", 2), ("QK", 5), ("QK", 6), ("VG", 3), ("ST", 1), ("VG", 4), ("VG", 5), ("QK", 7), ("VG", 6),
    ("VG", 7)]
ACT_FIRST = [("W2P", 0), ("ST", 0), ("VG", 0), ("VG", 1), ("SN", 0), ("VG", 2), ("SN", 1), ("VG", 3), ("VG", 4),
    ("ST", 1), ("VG", 5), ("QKHI", 0), ("VG", 6), ("VG", 7), ("CS", 0), ("CS", 1)]
POOL_FIRST = [("QK", 0), ("QK", 1), ("QK", 2), ("SN", 0), ("QK", 3), ("QK", 4), ("SN", 1), ("QK", 5), ("QK", 6),
    ("QKLO", 0), ("QK", 7)]
PROJECTING = {"QK", "VG", "ST", "SN", "CS", "W2P", "VGHI", "VGLO", "QKHI", "QKLO"}


def turns(orders, i, attend, project, split_qk, split_vg):
    usual, first, last = orders
    order = first if not attend else usual if project else last
    for step, n in order:
        if step in ("QKHI", "QKLO") and not split_qk or step in ("VGHI", "VGLO") and not split_vg:
            continue
        if (project if step in PROJECTING else attend):
            yield step, n


def every_turn(engine, run, before_loop=lambda: None):
    run(-1, attend=False, project=True, split_qk=True, split_vg=False)
    before_loop()
    with engine.Fori(0, PAIRS - 2) as i:
        run(i, attend=True, project=True, split_qk=True, split_vg=True)
    run(PAIRS - 2, attend=True, project=True, split_qk=False, split_vg=True)
    run(PAIRS - 1, attend=True, project=False, split_qk=False, split_vg=False)


def split_product(pe, out, w_hi, w_lo, m_hi, m_lo, first=True, last=True):
    pe.matmul(out, w_hi, m_hi, start=first, stop=False)
    pe.matmul(out, w_hi, m_lo, start=False, stop=False)
    return pe.matmul(out, w_lo, m_hi, start=False, stop=last)


def bank(ps, a, b, k):
    return ps[:, a:b].rearrange("p (k c) -> p k c", k=k)


class Norm:

    def __init__(self, nc, ctx, banks, xs, hn, ht_hi, ht_lo, ident, name):
        sb = lambda n, s: ctx.enter_context(nc.sbuf_tensor(f"{name}_{n}", s, F32))
        sem = lambda n: ctx.enter_context(nc.semaphore(f"{name}_{n}"))
        self.banks, self.xs, self.hn, self.ht_hi, self.ht_lo, self.ident = banks, xs, hn, ht_hi, ht_lo, ident
        self.stats, self.mv = sb("stats", [P, SEQS, 6]), sb("mv", [P, SEQS, 2])
        self.var_eps, self.rstd, self.minus_half = sb("var_eps", [P, SEQS, 1]), sb("rstd", [P, SEQS, 1]), sb("minus_half", [P, SEQS])
        self.stats_done, self.mv_done, self.var_done = sem("stats_done"), sem("mv_done"), sem("var_done")
        self.half_set, self.rstd_done, self.hn_done = sem("half_set"), sem("rstd_done"), sem("hn_done")
        self.turned, self.hi_done, self.lo_done = sem("turned"), sem("hi_done"), sem("lo_done")

    def vector_stats(self, dve, x_in):
        for half in range(2):
            seqs = slice(4 * half, 4 * half + 4)
            dve.wait_ge(x_in[half], 16)
            for b in range(4 * half, 4 * half + 4):
                dve.bn_stats(out=self.stats[:, b, :], in_=self.xs[:, b, :]).then_inc(self.stats_done, 1)
            for b in range(4 * half, 4 * half + 4):
                dve.wait_ge(self.stats_done, b + 1)
                dve.bn_aggr(out=self.mv[:, b, :], in_=self.stats[:, b, :]).then_inc(self.mv_done, 1)
            dve.wait_ge(self.mv_done, 4 * half + 4)
            dve.tensor_scalar(self.var_eps[:, seqs, 0], self.mv[:, seqs, 1], EPS, None, ALU.add).then_inc(self.var_done, 1)

    def vector_norm(self, dve, half):
        dve.wait_ge(self.rstd_done, half + 1)
        for b in range(4 * half, 4 * half + 4):
            dve.tensor_scalar(self.hn[:, b, :], self.xs[:, b, :], self.mv[:, b, 0:1], self.rstd[:, b, 0:1],
                              ALU.subtract, ALU.mult).then_inc(self.hn_done, 1)

    def pool(self, pool):
        pool.memset(self.minus_half[:, :], -0.5).then_inc(self.half_set, 1)
        pool.wait_ge(self.half_set, 1)
        for half in range(2):
            seqs = slice(4 * half, 4 * half + 4)
            pool.wait_ge(self.var_done, half + 1)
            pool.tensor_tensor(self.rstd[:, seqs, 0], self.var_eps[:, seqs, 0], self.minus_half[:, seqs], ALU.pow).then_inc(self.rstd_done, 1)

    def tensor(self, pe, normalised_here=True):
        for half in range(2):
            if normalised_here:
                pe.wait_ge(self.hn_done, 4 * half + 4)
            for kc in range(KC):
                for b in range(4):
                    mm = pe.transpose(self.banks[2 * half + kc][:, b * TOK:(b + 1) * TOK],
                                      self.hn[:, 4 * half + b, kc * P:(kc + 1) * P], self.ident)
                mm.then_inc(self.turned, 1)

    def scalar(self, act):
        for n in range(4):
            half, kc = n // 2, n % 2
            act.wait_ge(self.turned, n + 1)
            act.activation(self.ht_hi[:, kc, half * HALF:(half + 1) * HALF], self.banks[n][:, :], ACT.Copy).then_inc(self.hi_done, 1)

    def vector_low(self, dve, steps=range(4)):
        for n in steps:
            half, kc = n // 2, n % 2
            cols = slice(half * HALF, (half + 1) * HALF)
            dve.wait_ge(self.hi_done, n + 1)
            dve.tensor_tensor(self.ht_lo[:, kc, cols], self.banks[n][:, :], self.ht_hi[:, kc, cols].bitcast(F32),
                              ALU.subtract).then_inc(self.lo_done, 1)


TWO_PI = 2 * np.pi
TWO_PI_HI = 6.28125
ROUNDER = 1.5 * 2 ** 23


class Rotary:

    def __init__(self, nc, ctx, con):
        sb = lambda n, s: ctx.enter_context(nc.sbuf_tensor(f"rotary_{n}", s, F32))
        sem = lambda n: ctx.enter_context(nc.semaphore(f"rotary_{n}"))
        self.con, self.pos = con, sb("pos", [P, SEQS, 2])
        self.angle, self.turns, self.trig = sb("angle", [P, 2, SEQS, 4]), sb("turns", [P, 2, SEQS, 4]), sb("trig", [P, 2, SEQS, 4])
        self.cos, self.sin = sb("cos", [P, SEQS, 4, 2]), sb("sin", [P, SEQS, 4, 2])
        self.pos_in, self.table, self.trig_done, self.tables_done = sem("pos_in"), sem("table"), sem("trig_done"), sem("tables_done")

    def vector_angles(self, dve):
        pos, angle, turns_, table = self.pos, self.angle, self.turns, self.table
        freq = self.con[:, C_FREQ:C_FREQ + 4].rearrange("p (a f) -> p a f", a=2)
        dve.wait_ge(self.pos_in, 16)
        for c in range(SEQS):
            dve.tensor_tensor(angle[:, 0, c, :].rearrange("p (a f) -> p a f", a=2), pos[:, c, :].unsqueeze(2).to_broadcast([P, 2, 2]),
                              freq, ALU.mult).then_inc(table, 1)
        n = SEQS
        dve.wait_ge(table, n)
        dve.tensor_scalar(angle[:, 1, :, :], angle[:, 0, :, :], np.pi / 2, None, ALU.add).then_inc(table, 1)
        dve.wait_ge(table, n + 1)
        dve.tensor_scalar(turns_[:, :, :, :], angle[:, :, :, :], 1 / TWO_PI, ROUNDER, ALU.mult, ALU.add).then_inc(table, 1)
        dve.wait_ge(table, n + 2)
        dve.tensor_scalar(turns_[:, :, :, :], turns_[:, :, :, :], ROUNDER, None, ALU.subtract).then_inc(table, 1)
        dve.wait_ge(table, n + 3)
        dve.scalar_tensor_tensor(out=angle[:, :, :, :], in0=turns_[:, :, :, :], scalar=-TWO_PI_HI, in1=angle[:, :, :, :],
                                 op0=ALU.mult, op1=ALU.add).then_inc(table, 1)
        dve.wait_ge(table, n + 4)
        dve.scalar_tensor_tensor(out=angle[:, :, :, :], in0=turns_[:, :, :, :], scalar=-(TWO_PI - TWO_PI_HI), in1=angle[:, :, :, :],
                                 op0=ALU.mult, op1=ALU.add).then_inc(table, 1)
        dve.wait_ge(table, n + 5)
        dve.tensor_scalar(angle[:, :, :, :], angle[:, :, :, :], -3.1415925, 3.1415925, ALU.max, ALU.min).then_inc(table, 1)

    def scalar(self, act):
        act.wait_ge(self.table, SEQS + 6)
        act.activation(self.trig[:, :, :, :], self.angle[:, :, :, :], ACT.Sin).then_inc(self.trig_done, 1)

    def vector_tables(self, dve):
        cos, sin, trig = self.cos, self.sin, self.trig
        dve.wait_ge(self.trig_done, 1)
        for c in range(2):
            dve.tensor_copy(cos[:, :, :, c], trig[:, 1, :, :]).then_inc(self.tables_done, 1)
            dve.tensor_scalar(sin[:, :, :, c], trig[:, 0, :, :], 2.0 * c - 1.0, None, ALU.mult).then_inc(self.tables_done, 1)
        dve.wait_ge(self.tables_done, 4)


def slot_attention(nc, banks, xs, hn, ht_hi, ht_lo, con, rotary, early, x_in, a):
    tri, tris = con[:, C_TRI:C_TRI + TOK], con[:, C_TRIS:C_TRIS + TOK]
    ident, cos, sin = con[:, C_ID:C_ID + P], con[:, C_COS:C_COS + TOK], con[:, C_SIN:C_SIN + TOK]

    with ExitStack() as ctx:
        def sb(name, shape, dt=F32):
            return ctx.enter_context(nc.sbuf_tensor("sa_" + name, shape, dt))

        def sem(name):
            return ctx.enter_context(nc.semaphore("sa_" + name))

        qk_raw, vg_raw = sb("qk_raw", [P, KC, 512]), sb("vg_raw", [P, KC, 512])
        qk_hi, qk_lo = sb("qk_hi", [P, KC, 512], F32R), sb("qk_lo", [P, KC, 512], F32R)
        vg_hi, vg_lo = sb("vg_hi", [P, KC, 512], F32R), sb("vg_lo", [P, KC, 512], F32R)
        wo_raw, wo = sb("wo_raw", [P, 2, DIM]), sb("wo", [P, 2, DIM])
        wo_hi, wo_lo = sb("wo_hi", [P, 2, DIM], F32R), sb("wo_lo", [P, 2, DIM], F32R)
        gnorm, half_gnorm = sb("gnorm", [P, 1]), sb("half_gnorm", [P, 1])
        ws1_raw, ws1_hi, ws1_lo = sb("ws1_raw", [P, KC, P]), sb("ws1_hi", [P, KC, P], F32R), sb("ws1_lo", [P, KC, P], F32R)
        ws2_raw, ws2, ws2_pair = sb("ws2_raw", [P, PAIRS, P]), sb("ws2", [P, PAIRS, P], F32R), sb("ws2_pair", [P, P], F32R)
        us = sb("us", [P, ALL], F32R)
        rope_cos, rope_sin = sb("rope_cos", [P, 2, HALF]), sb("rope_sin", [P, 2, HALF])
        qt, kt = sb("qt", [P, 2, ALL]), sb("kt", [P, 2, ALL])
        v, gate, th = sb("v", [P, SEQS, 2 * DK]), sb("gate", [P, SEQS, 2 * DK]), sb("th", [P, 2, 2 * DK])
        u_full = gate[:, 0:4, :].rearrange("p b c -> p (b c)")
        st, sn = sb("st", [P, 2, HALF]), sb("sn", [P, 2, HALF])
        es, es_t = sb("es", [P, SEQS, 2 * SLOTS]), sb("es_t", [P, 2, ALL])
        es_hi, es_lo, tri_r = sb("es_hi", [P, 2, HALF], F32R), sb("es_lo", [P, 2, HALF], F32R), sb("tri_r", [P, TOK], F32R)
        log_cs, enz = sb("log_cs", [P, 2, HALF]), sb("enz", [P, SEQS, 2 * SLOTS])
        att, okb, ex = sb("att", [P, 2, 4, TOK]), sb("okb", [P, 2, 4, SLOTS]), sb("ex", [P, 2, 4, SLOTS])
        qe, qet, w2t = sb("qe", [P, 2, 4, SLOTS]), sb("qet", [P, 2, 2, TOK]), sb("w2t", [P, 2, 4, TOK])
        ogt_hi, ogt_lo = sb("ogt_hi", [P, 2, 4, TOK], F32R), sb("ogt_lo", [P, 2, 4, TOK], F32R)
        og, junk = sb("og", [P, 2, 4, DK]), sb("junk", [P, 4, DK])
        top, total, eps_t2 = sb("top", [P, 2, 4]), sb("total", [P, 4, 4]), sb("eps_t2", [P, 4, 4])
        ss, msq, rms = sb("ss", [P, 2, 4]), sb("msq", [P, 2, 4]), sb("rms", [P, 2, 4])
        minus_half, stats2, var2 = sb("minus_half", [P, 4]), sb("stats2", [P, SEQS, 6]), sb("var2", [P, SEQS])

        norm = Norm(nc, ctx, banks, xs, hn, ht_hi, ht_lo, ident, "norm1")
        con_in, ws1_in, ws2_in, gnorm_in, wo_in = sem("con_in"), sem("ws1_in"), sem("ws2_in"), sem("gnorm_in"), sem("wo_in")
        qk_in, vg_in = sem("qk_in"), sem("vg_in")
        ws1_hi_done, ws1_lo_done, ws2_hi_done, ws2_done = sem("ws1_hi_done"), sem("ws1_lo_done"), sem("ws2_hi_done"), sem("ws2_done")
        qk_hi_done, qk_lo_done, vg_hi_done, vg_lo_done = sem("qk_hi_done"), sem("qk_lo_done"), sem("vg_hi_done"), sem("vg_lo_done")
        u_ready, u_full_done, us_done = sem("u_ready"), sem("u_full_done"), sem("us_done")
        es_hi_done, es_lo_done, tri_done = sem("es_hi_done"), sem("es_lo_done"), sem("tri_done")
        wo_hi_done, wo_lo_done, ogt_lo_done = sem("wo_hi_done"), sem("wo_lo_done"), sem("ogt_lo_done")
        wo_scaled, zeros_set, half_set, pair_done = sem("wo_scaled"), sem("zeros_set"), sem("half_set"), sem("pair_done")
        fill, drain, summed = sem("fill"), sem("drain"), sem("summed")
        rope_parts, roped, v_done, th_done = sem("rope_parts"), sem("roped"), sem("v_done"), sem("th_done")
        es_t_done, es_done, enz_done = sem("es_t_done"), sem("es_done"), sem("enz_done")
        a_ready, e_ready, t_ready, w_ready = sem("a_ready"), sem("e_ready"), sem("t_ready"), sem("w_ready")
        o_ready, ot_ready, y_ready = sem("o_ready"), sem("ot_ready"), sem("y_ready")
        masked, scaled, topped, shifted = sem("masked"), sem("scaled"), sem("topped"), sem("shifted")
        totalled, eps_done, w2_done, msq_done = sem("totalled"), sem("eps_done"), sem("w2_done"), sem("msq_done")
        og_done, added = sem("og_done"), sem("added")
        exp_done, qet_done, squared, ogt_done = sem("exp_done"), sem("qet_done"), sem("squared"), sem("ogt_done")
        qe_done, rms_done = sem("qe_done"), sem("rms_done")
        stats2_done, mv2_done, var2_done = sem("stats2_done"), sem("mv2_done"), sem("var2_done")

        ps_a, ps_e, ps_t, ps_w, ps_y = banks[2], banks[3], banks[4], banks[5], banks[3]
        ps_o = banks[6:8]

        block = ctx.enter_context(nc.Block())

        @block.sync
        def _(sp):
            sp.dma_start(xs[:, 0:4, :], a["x"][0:4].rearrange("b t d -> t b d")).then_inc(x_in[0], 16)
            sp.dma_start(con[:, :], a["constants"]).then_inc(con_in, 16)
            sp.dma_start(xs[:, 4:8, :], a["x"][4:8].rearrange("b t d -> t b d")).then_inc(x_in[1], 16)
            sp.dma_start(rotary.pos[:, :, :], a["pos"].rearrange("b t p -> t b p")).then_inc(rotary.pos_in, 16)
            sp.dma_start(ws1_raw[:, :, :], a["ws1"]).then_inc(ws1_in, 16)
            sp.dma_start(qk_raw[:, :, :], a["wqk"][0]).then_inc(qk_in, 16)
            sp.dma_start(ws2_raw[:, :, :], a["ws2"]).then_inc(ws2_in, 16)
            sp.dma_start(vg_raw[:, :, :], a["wvg"][0]).then_inc(vg_in, 16)
            sp.dma_start(gnorm[:, :], a["g_norm"]).then_inc(gnorm_in, 16)
            sp.dma_start(wo_raw[:, :, :], a["wo"][0]).then_inc(wo_in, 16)
            sp.wait_ge(qk_lo_done, 1)
            sp.dma_start(qk_raw[:, :, :], a["wqk"][1]).then_inc(qk_in, 16)
            sp.wait_ge(vg_lo_done, 1)
            sp.dma_start(vg_raw[:, :, :], a["wvg"][1]).then_inc(vg_in, 16)
            with sp.Fori(0, PAIRS - 2) as i:
                sp.wait_ge(vg_lo_done, i + 2)
                sp.dma_start(vg_raw[:, :, :], a["wvg"][i + 2]).then_inc(vg_in, 16)
                sp.wait_ge(wo_scaled, i + 2)
                sp.dma_start(wo_raw[:, :, :], a["wo"][i + 1]).then_inc(wo_in, 16)
                sp.wait_ge(qk_lo_done, i + 2)
                sp.dma_start(qk_raw[:, :, :], a["wqk"][i + 2]).then_inc(qk_in, 16)
            sp.wait_ge(wo_scaled, PAIRS)
            sp.dma_start(wo_raw[:, :, :], a["wo"][PAIRS - 1]).then_inc(wo_in, 16)
            sp.dma_start(early["wkv"][:, :], a["wkv"]).then_inc(early["par_in"], 16)
            sp.dma_start(early["ctx_all"][:, :, :], a["ctx_t"].rearrange("b c t -> c b t")).then_inc(early["ctx_in"], 16)

        @block.tensor
        def _(pe):
            for s in (a_ready, e_ready, t_ready, w_ready, o_ready, ot_ready, y_ready):
                pe.sem_inc(s, LEAD)
            pe.wait_ge(con_in, 16)
            norm.tensor(pe)
            pe.wait_ge(norm.hi_done, 4)
            pe.wait_ge(norm.lo_done, 4)
            pe.wait_ge(ws1_lo_done, 1)
            for half in range(2):
                cols = slice(half * HALF, (half + 1) * HALF)
                for kc in range(KC):
                    mm = split_product(pe, banks[4 + half][:, :], ws1_hi[:, kc, :], ws1_lo[:, kc, :],
                                       ht_hi[:, kc, cols], ht_lo[:, kc, cols], kc == 0, kc == KC - 1)
                mm.then_inc(u_ready, 1)

            def run(i, attend, project, split_qk, split_vg):
                r = i + 1
                for step, n in turns((PE_ORDER, PE_ORDER, PE_LAST), i, attend, project, split_qk, split_vg):
                    g = n
                    if step in PROJECTING:
                        place = PLACE[step, n]
                        ps = banks[fill_bank(place, attend)]
                        if not attend:
                            if last_use(place) is not None:
                                pe.wait_ge(drain, last_use(place) + 1)
                        elif place >= 2:
                            pe.wait_ge(drain, NDRAIN * r + place - 1)
                        else:
                            pe.wait_ge(summed, 2 * r - 1 + place)
                    if step == "A":
                        if g % 2 == 0:
                            pe.wait_ge(roped, 8 * i + 4 * (g // 2) + 4)
                        pe.wait_ge(masked, at(i, g - 1))
                        for u in range(4):
                            b, h = 2 * g + u // 2, u % 2
                            mm = pe.matmul(ps_a[:, u * TOK:(u + 1) * TOK], kt[:, h, b * TOK:(b + 1) * TOK],
                                           qt[:, h, b * TOK:(b + 1) * TOK], start=True, stop=True)
                        mm.then_inc(a_ready, 1)
                    elif step == "E":
                        pe.wait_ge(masked, at(i, g))
                        pe.wait_ge(scaled, at(i, g - 1))
                        if g == 0:
                            pe.wait_ge(added, at(i, -1))
                        for u in range(4):
                            b, h = 2 * g + u // 2, u % 2
                            mm = pe.matmul(ps_e[:, u * SLOTS:(u + 1) * SLOTS], att[:, g % 2, u, :],
                                           es[:, b, h * SLOTS:(h + 1) * SLOTS], start=True, stop=True)
                        mm.then_inc(e_ready, 1)
                    elif step == "T":
                        pe.wait_ge(qe_done, at(i, g))
                        if g == 0:
                            pe.wait_ge(ogt_lo_done, at(i, -1))
                        else:
                            pe.wait_ge(qet_done, at(i, g - 1))
                        for b in range(2):
                            mm = pe.transpose(ps_t[:, b * TOK:(b + 1) * TOK],
                                              qe[:, g % 2, 2 * b:2 * b + 2, :].rearrange("p h m -> p (h m)"), ident)
                        mm.then_inc(t_ready, 1)
                    elif step == "W":
                        pe.wait_ge(qet_done, at(i, g))
                        pe.wait_ge(w2_done, at(i, g - 1))
                        for u in range(4):
                            b, h = 2 * g + u // 2, u % 2
                            mm = pe.matmul(ps_w[:, u * TOK:(u + 1) * TOK], es_t[:, h, b * TOK:(b + 1) * TOK],
                                           qet[:, g % 2, u // 2, :], start=True, stop=True)
                        mm.then_inc(w_ready, 1)
                    elif step == "O":
                        pe.wait_ge(w2_done, at(i, g))
                        pe.wait_ge(v_done, 8 * i + 2 * g + 2)
                        pe.wait_ge(og_done, at(i, g - 2))
                        for u in range(4):
                            b, h = 2 * g + u // 2, u % 2
                            mm = pe.matmul(ps_o[g % 2][:, u * DK:(u + 1) * DK], w2t[:, g % 2, u, :],
                                           v[:, b, h * DK:(h + 1) * DK], start=True, stop=True)
                        mm.then_inc(o_ready, 1)
                    elif step == "OT":
                        pe.wait_ge(og_done, at(i, g))
                        if g == 0:
                            pe.wait_ge(qet_done, at(i, 3))
                        else:
                            pe.wait_ge(ogt_lo_done, at(i, g - 1))
                        for u in range(4):
                            mm = pe.transpose(ps_t[:, u * TOK:(u + 1) * TOK], og[:, g % 2, u, :], ident)
                        mm.then_inc(ot_ready, 1)
                    elif step == "Y":
                        pe.wait_ge(ogt_lo_done, at(i, g))
                        pe.wait_ge(added, at(i, g - 1))
                        if g == 0:
                            pe.wait_ge(scaled, at(i, 3))
                            pe.wait_ge(wo_lo_done, i + 2)
                        for b in range(2):
                            for h in range(2):
                                u = 2 * b + h
                                mm = split_product(pe, ps_y[:, b * DIM:(b + 1) * DIM], ogt_hi[:, g % 2, u, :], ogt_lo[:, g % 2, u, :],
                                                   wo_hi[:, h, :], wo_lo[:, h, :], h == 0, h == 1)
                        mm.then_inc(y_ready, 1)
                    elif step == "QK":
                        c, j = n // 4, n % 4
                        if n == 0:
                            pe.wait_ge(qk_lo_done, r + 1)
                        cols, w = slice(c * HALF, (c + 1) * HALF), slice(j * DK, (j + 1) * DK)
                        for kc in range(KC):
                            mm = split_product(pe, ps[:, :], qk_hi[:, kc, w], qk_lo[:, kc, w],
                                               ht_hi[:, kc, cols], ht_lo[:, kc, cols], kc == 0, kc == KC - 1)
                        mm.then_inc(fill, 1)
                    elif step == "VG":
                        if n == 0:
                            pe.wait_ge(vg_lo_done, r + 1)
                        cols = slice(n * TOK, (n + 1) * TOK)
                        for kc in range(KC):
                            mm = split_product(pe, ps[:, :], ht_hi[:, kc, cols], ht_lo[:, kc, cols],
                                               vg_hi[:, kc, :], vg_lo[:, kc, :], kc == 0, kc == KC - 1)
                        mm.then_inc(fill, 1)
                    elif step == "ST":
                        if not attend:
                            pe.wait_ge(us_done, 4)
                        pe.wait_ge(pair_done, r + 1)
                        pe.matmul(ps[:, :], ws2_pair[:, :], us[:, n * HALF:(n + 1) * HALF],
                                  start=True, stop=True).then_inc(fill, 1)
                    elif step == "SN":
                        if not attend:
                            pe.wait_ge(us_done, 4)
                        pe.wait_ge(pair_done, r + 1)
                        for b in range(4):
                            mm = pe.matmul(ps[:, b * P:(b + 1) * P], us[:, (4 * n + b) * TOK:(4 * n + b + 1) * TOK],
                                           ws2_pair[:, :], start=True, stop=True)
                        mm.then_inc(fill, 1)
                    elif step == "CS":
                        if not attend:
                            pe.wait_ge(tri_done, 1)
                        pe.wait_ge(es_lo_done, 2 * r + n + 1)
                        pe.matmul(ps[:, :], tri_r[:, :], es_hi[:, n, :], start=True, stop=False)
                        pe.matmul(ps[:, :], tri_r[:, :], es_lo[:, n, :], start=False, stop=True).then_inc(fill, 1)

            every_turn(pe, run)

        @block.vector
        def _(dve):
            for s in (ogt_lo_done, masked, scaled, topped, shifted, totalled, eps_done, w2_done, msq_done, og_done, added):
                dve.sem_inc(s, LEAD)
            norm.vector_stats(dve, x_in)
            norm.vector_norm(dve, 0)
            norm.vector_norm(dve, 1)
            dve.wait_ge(ws1_hi_done, 1)
            dve.tensor_tensor(ws1_lo[:, :, :], ws1_raw[:, :, :], ws1_hi[:, :, :].bitcast(F32), ALU.subtract).then_inc(ws1_lo_done, 1)
            norm.vector_low(dve)
            dve.wait_ge(con_in, 16)
            dve.wait_ge(ws2_hi_done, 1)
            dve.scalar_tensor_tensor(out=ws2[:, :, :], in0=ws2[:, :, :].bitcast(F32), scalar=con[:, C_LOW_W:C_LOW_W + 1],
                                     in1=ws2_raw[:, :, :], op0=ALU.mult, op1=ALU.add).then_inc(ws2_done, 1)
            for half in range(2):
                cols = slice(half * HALF, (half + 1) * HALF)
                dve.wait_ge(u_ready, half + 1)
                dve.tensor_scalar(u_full[:, cols], banks[4 + half][:, :], con[:, C_ONE:C_ONE + 1], None, ALU.add).then_inc(u_full_done, 1)
                dve.wait_ge(u_full_done, half + 1)
                dve.tensor_copy(us[:, cols], u_full[:, cols]).then_inc(us_done, 1)
                dve.wait_ge(us_done, 2 * half + 1)
                dve.scalar_tensor_tensor(out=us[:, cols], in0=us[:, cols].bitcast(F32), scalar=con[:, C_LOW_U:C_LOW_U + 1],
                                         in1=u_full[:, cols], op0=ALU.mult, op1=ALU.add).then_inc(us_done, 1)

            def run(i, attend, project, split_qk, split_vg):
                r = i + 1
                for step, n in turns((DVE_ORDER, DVE_FIRST, DVE_LAST), i, attend, project, split_qk, split_vg):
                    g, s = n, n % 2
                    if step in PROJECTING:
                        ps = banks[fill_bank(PLACE[step, n], attend)]
                        dve.wait_ge(fill, filled(r, (step, n)))
                    if step == "A":
                        dve.wait_ge(a_ready, at(i, g))
                        dve.wait_ge(e_ready, at(i, g - 2))
                        dve.tensor_tensor(att[:, s, :, :], bank(ps_a, 0, 512, 4),
                                          tris.unsqueeze(1).to_broadcast([P, 4, TOK]), ALU.mult).then_inc(masked, 1)
                    elif step == "E":
                        dve.wait_ge(e_ready, at(i, g))
                        dve.wait_ge(enz_done, 2 * i + g // 2 + 1)
                        dve.wait_ge(exp_done, at(i, g - 2))
                        dve.tensor_tensor(okb[:, s, :, :], bank(ps_e, 0, 256, 4),
                                          enz[:, 2 * g:2 * g + 2, :].rearrange("p b (h m) -> p (b h) m", h=2), ALU.mult).then_inc(scaled, 1)
                        dve.wait_ge(scaled, at(i, g))
                        dve.tensor_reduce(top[:, s, :], okb[:, s, :, :], AX.X, ALU.max).then_inc(topped, 1)
                        dve.wait_ge(topped, at(i, g))
                        dve.tensor_tensor(okb[:, s, :, :], okb[:, s, :, :],
                                          top[:, s, :].unsqueeze(2).to_broadcast([P, 4, SLOTS]), ALU.subtract).then_inc(shifted, 1)
                    elif step == "SUM":
                        dve.wait_ge(exp_done, at(i, g))
                        dve.tensor_reduce(total[:, g, :], ex[:, s, :, :], AX.X, ALU.add).then_inc(totalled, 1)
                        dve.wait_ge(totalled, at(i, g))
                        dve.wait_ge(msq_done, at(i, g - 4))
                        dve.scalar_tensor_tensor(out=eps_t2[:, g, :], in0=total[:, g, :], scalar=EPS, in1=total[:, g, :],
                                                 op0=ALU.mult, op1=ALU.mult).then_inc(eps_done, 1)
                    elif step == "W":
                        dve.wait_ge(w_ready, at(i, g))
                        dve.wait_ge(o_ready, at(i, g - 2))
                        dve.tensor_tensor(w2t[:, s, :, :], bank(ps_w, 0, 512, 4),
                                          tri.unsqueeze(1).to_broadcast([P, 4, TOK]), ALU.mult).then_inc(w2_done, 1)
                    elif step == "MS":
                        dve.wait_ge(squared, at(i, g))
                        dve.wait_ge(eps_done, at(i, g))
                        dve.wait_ge(rms_done, at(i, g - 2))
                        dve.scalar_tensor_tensor(out=msq[:, s, :], in0=ss[:, s, :], scalar=1.0 / DK, in1=eps_t2[:, g, :],
                                                 op0=ALU.mult, op1=ALU.add).then_inc(msq_done, 1)
                    elif step == "O":
                        dve.wait_ge(rms_done, at(i, g))
                        dve.wait_ge(drain, drained(i, ("VG", 2 * g + 1)))
                        dve.wait_ge(ot_ready, at(i, g - 2))
                        for u in range(4):
                            b, h = 2 * g + u // 2, u % 2
                            ins = dve.scalar_tensor_tensor(out=og[:, s, u, :], in0=ps_o[s][:, u * DK:(u + 1) * DK],
                                                           scalar=rms[:, s, u:u + 1], in1=gate[:, b, h * DK:(h + 1) * DK],
                                                           op0=ALU.mult, op1=ALU.mult)
                        ins.then_inc(og_done, 1)
                    elif step == "OT":
                        dve.wait_ge(ogt_done, at(i, g))
                        dve.wait_ge(y_ready, at(i, g - 2))
                        dve.tensor_tensor(ogt_lo[:, s, :, :], bank(ps_t, 0, 512, 4), ogt_hi[:, s, :, :].bitcast(F32),
                                          ALU.subtract).then_inc(ogt_lo_done, 1)
                    elif step == "Y":
                        dve.wait_ge(y_ready, at(i, g))
                        dve.wait_ge(added, at(i, g - 1))
                        dve.tensor_tensor(xs[:, 2 * g:2 * g + 2, :], bank(ps_y, 0, 512, 2), xs[:, 2 * g:2 * g + 2, :],
                                          ALU.add).then_inc(added, 1)
                    elif step == "N2":
                        dve.wait_ge(added, at(i, g))
                        for b in range(2 * g, 2 * g + 2):
                            dve.bn_stats(out=stats2[:, b, :], in_=xs[:, b, :]).then_inc(stats2_done, 1)
                        for b in range(2 * g, 2 * g + 2):
                            dve.wait_ge(stats2_done, b + 1)
                            dve.bn_aggr(out=early["mv"][:, b, :], in_=stats2[:, b, :]).then_inc(mv2_done, 1)
                        dve.wait_ge(mv2_done, 2 * g + 2)
                        dve.tensor_scalar(var2[:, 2 * g:2 * g + 2], early["mv"][:, 2 * g:2 * g + 2, 1], EPS, None, ALU.add).then_inc(var2_done, 1)
                    elif step == "QK":
                        if attend or n >= 2:
                            dve.wait_ge(roped, 8 * r + n - 1)
                        cos4 = cos.unsqueeze(1).to_broadcast([P, 4, TOK])
                        sin4 = sin.unsqueeze(1).to_broadcast([P, 4, TOK])
                        psv = bank(ps, 0, 512, 4)
                        rs = rope_sin[:, s, :].rearrange("p (b t) -> p b t", b=4)
                        dve.tensor_tensor(rope_cos[:, s, :].rearrange("p (b t) -> p b t", b=4), psv, cos4, ALU.mult)
                        dve.tensor_tensor(rs[0:64], psv[64:128], sin4[64:128], ALU.mult)
                        dve.tensor_tensor(rs[64:128], psv[0:64], sin4[0:64], ALU.mult).then_inc(drain, 1)
                    elif step == "VG":
                        dve.wait_ge(th_done, 8 * r + n + 1)
                        if attend:
                            dve.wait_ge(og_done, at(i, n // 2))
                        dve.scalar_tensor_tensor(out=gate[:, n, :], in0=th[:, s, :], scalar=1.0, in1=ps[:, 256:512],
                                                 op0=ALU.add, op1=ALU.mult).then_inc(drain, 1)
                    elif step in ("ST", "SN"):
                        dst, done = (st, es_t_done) if step == "ST" else (sn, es_done)
                        if attend:
                            dve.wait_ge(done, 2 * r + n - 1)
                        dve.tensor_scalar(dst[:, n, :], ps[:, :], -CLAMP, CLAMP, ALU.max, ALU.min).then_inc(drain, 1)

            every_turn(dve, run, before_loop=lambda: (rotary.vector_angles(dve), rotary.vector_tables(dve)))

        @block.scalar
        def _(act):
            for s in (exp_done, qet_done, squared, ogt_done):
                act.sem_inc(s, LEAD)
            act.sem_inc(wo_hi_done, 1)
            act.wait_ge(con_in, 16)
            act.wait_ge(ws1_in, 16)
            act.activation(tri_r[:, :], tri, ACT.Copy).then_inc(tri_done, 1)
            act.activation(ws1_hi[:, :, :], ws1_raw[:, :, :], ACT.Copy).then_inc(ws1_hi_done, 1)
            act.wait_ge(qk_in, 16)
            act.activation(qk_hi[:, :, :], qk_raw[:, :, :], ACT.Copy).then_inc(qk_hi_done, 1)
            norm.scalar(act)
            act.wait_ge(ws2_in, 16)
            act.activation(ws2[:, :, :], ws2_raw[:, :, :], ACT.Copy).then_inc(ws2_hi_done, 1)
            act.wait_ge(vg_in, 16)
            act.activation(vg_hi[:, :, :], vg_raw[:, :, :], ACT.Copy).then_inc(vg_hi_done, 1)
            act.wait_ge(ws2_done, 1)

            def run(i, attend, project, split_qk, split_vg):
                r = i + 1
                for step, n in turns((ACT_ORDER, ACT_FIRST, ACT_LAST), i, attend, project, split_qk, split_vg):
                    g, s = n, n % 2
                    if (step, n) == ("CS", 0):
                        act.preload_act_table_set("natural_log_exp_and_others")
                    if step in ("VG", "CS"):
                        ps = banks[fill_bank(PLACE[step, n], attend)]
                        act.wait_ge(fill, filled(r, (step, n)))
                    if step == "W2P":
                        if attend:
                            act.wait_ge(fill, filled(i, ("SN", 1)))
                        act.activation(ws2_pair[:, :], ws2[:, r, :].bitcast(F32), ACT.Copy).then_inc(pair_done, 1)
                    elif step == "VGHI":
                        act.wait_ge(vg_in, 16 * r + 16)
                        act.wait_ge(fill, filled(i, ("VG", 7)))
                        act.activation(vg_hi[:, :, :], vg_raw[:, :, :], ACT.Copy).then_inc(vg_hi_done, 1)
                    elif step == "QKHI":
                        act.wait_ge(qk_in, 16 * r + 32)
                        act.wait_ge(fill, filled(r, ("QK", 7)))
                        act.activation(qk_hi[:, :, :], qk_raw[:, :, :], ACT.Copy).then_inc(qk_hi_done, 1)
                    elif step == "E":
                        act.wait_ge(shifted, at(i, g))
                        act.wait_ge(qe_done, at(i, g - 2))
                        act.wait_ge(totalled, at(i, g - 2))
                        act.activation(ex[:, s, :, :], okb[:, s, :, :], ACT.Exp).then_inc(exp_done, 1)
                    elif step == "T":
                        act.wait_ge(t_ready, at(i, g))
                        act.wait_ge(w_ready, at(i, g - 2))
                        act.activation(qet[:, s, :, :], bank(ps_t, 0, 256, 2), ACT.Copy).then_inc(qet_done, 1)
                    elif step == "O":
                        act.wait_ge(o_ready, at(i, g))
                        act.wait_ge(msq_done, at(i, g - 2))
                        act.wait_ge(squared, at(i, g - 1))
                        for u in range(4):
                            ins = act.activation(junk[:, u, :], ps_o[s][:, u * DK:(u + 1) * DK], ACT.Square,
                                                 accum_out=ss[:, s, u:u + 1])
                        ins.then_inc(squared, 1)
                    elif step == "OT":
                        act.wait_ge(ot_ready, at(i, g))
                        act.wait_ge(y_ready, at(i, g - 2))
                        act.activation(ogt_hi[:, s, :, :], bank(ps_t, 0, 512, 4), ACT.Copy).then_inc(ogt_done, 1)
                    elif step == "WOHI":
                        act.wait_ge(wo_scaled, i + 2)
                        act.wait_ge(y_ready, at(i, -1))
                        act.activation(wo_hi[:, :, :], wo[:, :, :], ACT.Copy).then_inc(wo_hi_done, 1)
                    elif step == "VG":
                        if attend:
                            act.wait_ge(o_ready, at(i, n // 2))
                        act.activation(v[:, n, :], ps[:, 0:256], ACT.Copy).then_inc(v_done, 1)
                        if attend or n >= 2:
                            prev = drained(r, ("VG", n - 2)) if n >= 2 else drained(i, ("VG", n + 6))
                            act.wait_ge(drain, prev)
                        act.activation(th[:, s, :], ps[:, 256:512], ACT.Tanh, scale=0.5).then_inc(th_done, 1)
                    elif step == "ST":
                        act.wait_ge(drain, drained(r, ("ST", n)))
                        if attend:
                            act.wait_ge(w_ready, at(i, 2 * n + 1))
                        cols = slice(n * HALF, (n + 1) * HALF)
                        if not attend:
                            act.wait_ge(zeros_set, 1)
                        act.activation(es_t[0:64, 0, cols], st[0:64, n, :], ACT.Exp)
                        act.activation(es_t[64:128, 1, cols], st[64:128, n, :], ACT.Exp).then_inc(es_t_done, 1)
                    elif step == "SN":
                        act.wait_ge(drain, drained(r, ("SN", n)))
                        if attend:
                            act.wait_ge(e_ready, at(i, 2 * n + 1))
                        act.activation(es[:, 4 * n:4 * n + 4, :], sn[:, n, :].rearrange("p (b m) -> p b m", b=4),
                                       ACT.Exp).then_inc(es_done, 1)
                        act.wait_ge(es_done, 2 * r + n + 1)
                        if attend:
                            act.wait_ge(fill, filled(i, ("CS", n)))
                        act.activation(es_hi[:, n, :].rearrange("p (b m) -> p b m", b=4), es[:, 4 * n:4 * n + 4, :],
                                       ACT.Copy).then_inc(es_hi_done, 1)
                    elif step == "CS":
                        if attend:
                            act.wait_ge(enz_done, 2 * r + n - 1)
                        act.activation(log_cs[:, n, :], ps[:, :], ACT.Ln).then_inc(summed, 1)
                        act.wait_ge(summed, 2 * r + n + 1)
                        if attend:
                            act.wait_ge(scaled, at(i, 2 * n + 1))
                            act.wait_ge(qe_done, at(i, 2 * n + 1))
                        act.activation(enz[:, 4 * n:4 * n + 4, :], log_cs[:, n, :].rearrange("p (b m) -> p b m", b=4),
                                       ACT.Exp, scale=-1.0).then_inc(enz_done, 1)

            every_turn(act, run, before_loop=lambda: rotary.scalar(act))

        @block.gpsimd
        def _(pool):
            for s in (qe_done, rms_done):
                pool.sem_inc(s, LEAD)
            pool.sem_inc(wo_scaled, 1)
            pool.sem_inc(wo_lo_done, 1)
            norm.pool(pool)
            pool.wait_ge(qk_hi_done, 1)
            pool.tensor_tensor(qk_lo[:, :, :], qk_raw[:, :, :], qk_hi[:, :, :].bitcast(F32), ALU.subtract).then_inc(qk_lo_done, 1)
            pool.memset(minus_half[:, :], -0.5).then_inc(half_set, 1)
            pool.memset(es_t[:, :, :], 0.0).then_inc(zeros_set, 1)
            pool.wait_ge(vg_hi_done, 1)
            pool.tensor_tensor(vg_lo[:, :, :], vg_raw[:, :, :], vg_hi[:, :, :].bitcast(F32), ALU.subtract).then_inc(vg_lo_done, 1)
            pool.wait_ge(gnorm_in, 16)
            pool.tensor_scalar(half_gnorm[:, :], gnorm[:, :], 0.5, None, ALU.mult).then_inc(half_set, 1)
            pool.wait_ge(half_set, 2)

            def run(i, attend, project, split_qk, split_vg):
                r = i + 1
                for step, n in turns((POOL_ORDER, POOL_FIRST, POOL_LAST), i, attend, project, split_qk, split_vg):
                    g, s = n, n % 2
                    if step == "QK":
                        c, h, dst = n // 4, n % 4 // 2, (qt, kt)[n % 2]
                        pool.wait_ge(drain, drained(r, ("QK", n)))
                        if attend:
                            pool.wait_ge(a_ready, at(i, 2 * c + 1))
                        pool.tensor_tensor(dst[:, h, c * HALF:(c + 1) * HALF], rope_cos[:, s, :], rope_sin[:, s, :],
                                           ALU.add).then_inc(roped, 1)
                    elif step == "E":
                        pool.wait_ge(exp_done, at(i, g))
                        pool.wait_ge(enz_done, 2 * i + g // 2 + 1)
                        pool.wait_ge(t_ready, at(i, g - 2))
                        pool.tensor_tensor(qe[:, s, :, :], ex[:, s, :, :],
                                           enz[:, 2 * g:2 * g + 2, :].rearrange("p b (h m) -> p (b h) m", h=2), ALU.mult).then_inc(qe_done, 1)
                    elif step == "MS":
                        pool.wait_ge(msq_done, at(i, g))
                        pool.wait_ge(og_done, at(i, g - 2))
                        pool.tensor_tensor(rms[:, s, :], msq[:, s, :], minus_half[:, :], ALU.pow).then_inc(rms_done, 1)
                    elif step == "SN":
                        pool.wait_ge(es_hi_done, 2 * r + n + 1)
                        if attend:
                            pool.wait_ge(fill, filled(i, ("CS", n)))
                        pool.tensor_tensor(es_lo[:, n, :].rearrange("p (b m) -> p b m", b=4), es[:, 4 * n:4 * n + 4, :],
                                           es_hi[:, n, :].bitcast(F32).rearrange("p (b m) -> p b m", b=4), ALU.subtract).then_inc(es_lo_done, 1)
                    elif step == "WO":
                        pool.wait_ge(wo_in, 16 * i + 16)
                        pool.wait_ge(wo_hi_done, i + 1)
                        pool.tensor_tensor(wo[:, :, :], wo_raw[:, :, :], half_gnorm[:, 0:1].unsqueeze(2).to_broadcast([P, 2, DIM]),
                                           ALU.mult).then_inc(wo_scaled, 1)
                    elif step == "WOLO":
                        pool.wait_ge(wo_hi_done, i + 2)
                        pool.wait_ge(y_ready, at(i, -1))
                        pool.tensor_tensor(wo_lo[:, :, :], wo[:, :, :], wo_hi[:, :, :].bitcast(F32), ALU.subtract).then_inc(wo_lo_done, 1)
                    elif step == "N2":
                        pool.wait_ge(var2_done, g + 1)
                        pool.tensor_tensor(early["rstd"][:, 2 * g:2 * g + 2, 0], var2[:, 2 * g:2 * g + 2], minus_half[:, 0:2], ALU.pow)
                    elif step == "VGLO":
                        pool.wait_ge(vg_hi_done, r + 1)
                        pool.tensor_tensor(vg_lo[:, :, :], vg_raw[:, :, :], vg_hi[:, :, :].bitcast(F32), ALU.subtract).then_inc(vg_lo_done, 1)
                    elif step == "QKLO":
                        pool.wait_ge(qk_hi_done, r + 2)
                        pool.tensor_tensor(qk_lo[:, :, :], qk_raw[:, :, :], qk_hi[:, :, :].bitcast(F32), ALU.subtract).then_inc(qk_lo_done, 1)

            every_turn(pool, run)


XHEADS, XDIM, CTX = 32, 8, 128
STACK = 32
XV = XDIM + 1
HG = XHEADS // 4
LEAD_B = 3

GT_KV, GT_H, GT_Q, GT_K, GT_QT, NG = 0, 1, 2, 3, 5, 7
G_ACT = {GT_H: 0, 3: 1, 4: 2, 5: 3, 6: 4}
G_DVE = {GT_KV: 0, GT_Q: 1}
X_PE = [("L2", 0), ("L2", 1), ("L1", 0), ("G", 0), ("L1", 1), ("AV", 0), ("L2", 2), ("L2", 3), ("AV", 1), ("G", 1),
    ("L2", 4), ("AV", 2), ("L1", 2), ("AV", 3), ("L1", 3), ("L2", 5), ("L2", 6), ("AV", 4), ("AB", 0), ("L1", 4),
    ("AV", 5), ("L2", 7), ("L1", 5), ("G", 2), ("AV", 6), ("AV", 7), ("L1", 6), ("L1", 7), ("G", 3), ("AB", 1),
    ("G", 4), ("AT", 0), ("M", 0), ("OUT", 0), ("G", 5), ("M", 1), ("G", 6)]
X_DVE = [("H", 0), ("L1", 0), ("L1", 1), ("G", 0), ("L1", 2), ("L1", 3), ("DV", 0), ("L1", 4), ("L1", 5), ("G", 2),
    ("L1", 6), ("L1", 7), ("DV", 1), ("NEG", 0), ("KD", 0), ("OUT", 0), ("S3", 0), ("M", 1), ("HN", 0), ("KD", 1)]
X_ACT = [("L2", 0), ("L2", 1), ("V", 0), ("L2", 2), ("L2", 3), ("SPLIT", 0), ("L2", 4), ("AC", 0), ("G", 1),
    ("L2", 5), ("L2", 6), ("HI", 0), ("L2", 7), ("AC", 1), ("G", 3), ("HI", 1), ("G", 4), ("AT", 0), ("M", 0),
    ("G", 5), ("G", 6), ("M", 1)]
X_POOL = [("CTX", 0), ("ROT", 0), ("LO", 0), ("SPLIT", 0), ("ROT", 1), ("BIAS", 0), ("LO", 1), ("S3", 0)]
STAGE_B, STAGE_C = {"L1", "NEG", "M", "SPLIT"}, {"L2", "AV", "AC", "AB", "DV", "AT", "OUT", "S3", "HN"}


def done(b, n=0, k=1):
    return k * (b + LEAD_B) + n + 1


def sequences(engine, run):
    run(-2, 1, "A")
    run(-1, 2, "AB")
    with engine.Fori(0, SEQS - 4, 3) as b:
        for s in range(3):
            run(b + s, s, "ABC")
    run(SEQS - 2, 0, "BC")
    run(SEQS - 1, 1, "C")


def stage_steps(order, turn, s, stages):
    for step, n in order:
        stage = "B" if step in STAGE_B else "C" if step in STAGE_C else "A"
        ahead = "CBA".index(stage)
        if stage in stages:
            yield step, n, turn + ahead, (s + ahead) % 3


def cross_attention(nc, banks, xs, hn, con, rotary, early, w, a):
    ident = con[:, C_ID:C_ID + P]

    with ExitStack() as ctx:
        def sb(name, shape, dt=F32):
            return ctx.enter_context(nc.sbuf_tensor("xa_" + name, shape, dt))

        def sem(name):
            return ctx.enter_context(nc.semaphore("xa_" + name))

        wq, wout = sb("wq", [P, KC, DIM]), sb("wout", [P, KC, DIM])
        wkv, ctx_all = early["wkv"], early["ctx_all"]
        bout = sb("bout", [P, DIM])
        mv, rstd, minus_half = early["mv"], early["rstd"], sb("minus_half", [P, 1])
        stats3, mv3, var_eps3, rstd3 = sb("stats3", [P, 6]), sb("mv3", [P, 2]), sb("var_eps3", [P, 1]), sb("rstd3", [P, 1])
        h2, h2t, ctx_b = sb("h2", [P, DIM]), sb("h2t", [P, KC, TOK]), sb("ctx_b", [P, TOK])
        by_cos, by_sin, rot = sb("by_cos", [P, 2, XHEADS, XDIM]), sb("by_sin", [P, 2, XHEADS, XDIM]), sb("rot", [P, 2, XHEADS, XDIM])
        stack = sb("stack", [P, 4, XHEADS, STACK])
        kt, qt = sb("kt", [P, 3, HG, TOK], F32R), sb("qt", [P, HG, TOK], F32R)
        k_diag, q_diag = sb("k_diag", [P, HG, 4, TOK], F32R), sb("q_diag", [P, HG, 4, TOK], F32R)
        va, avt = sb("va", [P, 3, XHEADS * XV + QUAD - XV]), sb("avt", [P, 2, 4, TOK])
        top = sb("top", [P, HG, 4])
        wt = sb("wt", [P, 2, 4, TOK])
        rsum, att, att_t = sb("rsum", [P, XHEADS]), sb("att", [P, DIM]), sb("att_t", [P, KC, TOK])

        cos, sin = rotary.cos, rotary.sin
        par_in, ctx_in, wq_in = early["par_in"], early["ctx_in"], sem("wq_in")
        wout_in, bout_in = sem("wout_in"), sem("bout_in")
        set_done, k_diag_set, q_diag_set = sem("set_done"), sem("k_diag_set"), sem("q_diag_set")
        norm3_sems = [sem(n) for n in ("stats3_done", "mv3_done", "var3_done", "hn_done")]
        stats3_done, mv3_done, var3_done, hn_done = norm3_sems
        rstd3_done, waited = sem("rstd3_done"), sem("waited")
        half_set, k_diag_done = sem("half_set"), sem("k_diag_done")
        m_act, m_dve, avt_done = sem("m_act"), sem("m_dve"), sem("avt_done")
        dve_sems = [sem(n) for n in ("h2_done", "neg_done", "rsum_done", "att_done", "added")]
        h2_done, neg_done, rsum_done, att_done, added = dve_sems
        g_dve, top_done = sem("g_dve"), sem("top_done")
        pe_g, pe_m, pe_l1, pe_l2, pe_av, pe_ab, pe_at, pe_out = [sem(n) for n in ("pe_g", "pe_m", "pe_l1", "pe_l2", "pe_av", "pe_ab", "pe_at", "pe_out")]
        g_act, exp_done, v_done, hi_done, att_t_done = [sem(n) for n in ("g_act", "exp_done", "v_done", "hi_done", "att_t_done")]
        ctx_done, rot_done, lo_done, bias_done = [sem(n) for n in ("ctx_done", "rot_done", "lo_done", "bias_done")]

        ps_g, ps_1, ps_2, ps_av, ps_m = banks[0:2], banks[2:4], banks[4:6], banks[6], banks[7]
        block = ctx.enter_context(nc.Block())

        @block.sync
        def _(sp):
            sp.dma_start(wq[:, :, :], a["xwq"]).then_inc(wq_in, 16)
            sp.dma_start(wout[:, :, :], a["wout"]).then_inc(wout_in, 16)
            sp.dma_start(bout[:, :], a["bout"].to_broadcast([P, DIM])).then_inc(bout_in, 16)
            sp.dma_start(w["w13_raw"][:, :, :, :], a["w13"]).then_inc(w["w13_in"], 16)
            sp.dma_start(w["gate_raw"][:, :, :], a["gate"]).then_inc(w["gate_in"], 16)
            sp.dma_start(w["w2"][:, :, :], a["w2"]).then_inc(w["w2_in"], 16)

        @block.tensor
        def _(pe):
            for s, k in ((pe_g, NG), (pe_m, 2), (pe_l1, 8), (pe_l2, 8), (pe_av, 8), (pe_ab, 2), (pe_at, 1), (pe_out, 1)):
                pe.sem_inc(s, k * LEAD_B)

            def turn_stack(ps, which, half):
                for j in range(4):
                    hg = 4 * half + j
                    mm = pe.transpose(ps[:, j * TOK:(j + 1) * TOK],
                                      stack[:, which, 4 * hg:4 * hg + 4, :].rearrange("p h c -> p (h c)"), ident)
                return mm

            def run(turn, s, stages):
                for step, n, b, p in stage_steps(X_PE, turn, s, stages):
                    if step == "G":
                        ps = ps_g[n % 2]
                        before = n - 2 if n >= 2 else (6, 5)[n]
                        last = b if n >= 2 else b - 1
                        if before in G_ACT:
                            pe.wait_ge(g_act, done(last, G_ACT[before], len(G_ACT)))
                        else:
                            pe.wait_ge(g_dve, done(last, G_DVE[before], len(G_DVE)))
                        if n == GT_KV:
                            pe.wait_ge(ctx_done, done(b))
                            if stages == "A":
                                pe.wait_ge(par_in, 16)
                            if stages == "AB":
                                pe.wait_ge(wout_in, 16)
                            mm = pe.matmul(ps[:, :], ctx_b[:, :], wkv[:, :], start=True, stop=True)
                        elif n == GT_H:
                            pe.wait_ge(h2_done, done(b))
                            for kc in range(KC):
                                mm = pe.transpose(ps[:, kc * TOK:(kc + 1) * TOK], h2[:, kc * P:(kc + 1) * P], ident)
                        elif n == GT_Q:
                            pe.wait_ge(g_act, done(b, G_ACT[GT_H], len(G_ACT)))
                            if stages == "A":
                                pe.wait_ge(wq_in, 16)
                            for kc in range(KC):
                                mm = pe.matmul(ps[:, 0:DIM], h2t[:, kc, :], wq[:, kc, :], start=(kc == 0), stop=(kc == KC - 1))
                        else:
                            which, half = (n - GT_K) // 2, (n - GT_K) % 2
                            pe.wait_ge(lo_done, done(b, which, 2))
                            if stages == "A":
                                pe.wait_ge(set_done, 3)
                            mm = turn_stack(ps, (0, 1 + p)[which], half)
                        mm.then_inc(pe_g, 1)
                    elif step == "M":
                        if n == 0:
                            pe.wait_ge(neg_done, done(b))
                        turn_stack(ps_1[n], 1 + p, n).then_inc(pe_m, 1)
                    elif step == "L1":
                        if n == 0:
                            pe.wait_ge(g_act, done(b, G_ACT[6], len(G_ACT)))
                        if n % 4 == 0:
                            pe.wait_ge(k_diag_done, done(b, n // 4, 2))
                        if n >= 2:
                            pe.wait_ge(top_done, done(b, n - 2, 8))
                        else:
                            pe.wait_ge(m_act, done(b - 1, n, 2))
                            if n == 1:
                                pe.wait_ge(m_dve, done(b - 1))
                        pe.matmul(ps_1[n % 2][:, :], qt[:, n, :], k_diag[:, n, :, :].rearrange("p h t -> p (h t)"),
                                  start=True, stop=True).then_inc(pe_l1, 1)
                    elif step == "L2":
                        if n % 4 == 0:
                            pe.wait_ge(m_act, done(b, n // 4, 2))
                            if n == 4:
                                pe.wait_ge(m_dve, done(b))
                        pe.wait_ge(exp_done, done(b, n - 2, 8) if n >= 2 else done(b - 1, n + 6, 8))
                        pe.matmul(ps_2[n % 2][:, :], kt[:, p, n, :], q_diag[:, n, :, :].rearrange("p h t -> p (h t)"),
                                  start=True, stop=True).then_inc(pe_l2, 1)
                    elif step == "AV":
                        pe.wait_ge(exp_done, done(b, n, 8))
                        if n == 0:
                            pe.wait_ge(att_done, done(b - 1, 0, 2))
                        if n == 4:
                            pe.wait_ge(added, done(b - 1))
                        for j in range(4):
                            col = (4 * n + j) * XV
                            mm = pe.matmul((ps_av, ps_m)[n // 4][j * QUAD:(j + 1) * QUAD, n % 4 * TOK:(n % 4 + 1) * TOK],
                                           va[:, p, col:col + QUAD], wt[:, n % 2, j, :], start=True, stop=True)
                        mm.then_inc(pe_av, 1)
                    elif step == "AB":
                        pe.wait_ge(avt_done, done(b, n, 2))
                        for j in range(4):
                            mm = pe.transpose((ps_av, ps_m)[n][:, j * TOK:(j + 1) * TOK], avt[:, n, j, :], ident)
                        mm.then_inc(pe_ab, 1)
                    elif step == "AT":
                        pe.wait_ge(att_done, done(b, 1, 2))
                        for kc in range(KC):
                            mm = pe.transpose(ps_m[:, kc * TOK:(kc + 1) * TOK], att[:, kc * P:(kc + 1) * P], ident)
                        mm.then_inc(pe_at, 1)
                    elif step == "OUT":
                        pe.wait_ge(att_t_done, done(b))
                        for kc in range(KC):
                            mm = pe.matmul(ps_m[:, 0:DIM], att_t[:, kc, :], wout[:, kc, :], start=(kc == 0), stop=(kc == KC - 1))
                        mm.then_inc(pe_out, 1)

            sequences(pe, run)

        @block.vector
        def _(dve):
            for s in dve_sems:
                dve.sem_inc(s, (2 if s in (rsum_done, att_done) else 1) * LEAD_B)
            for s in norm3_sems:
                dve.sem_inc(s, LEAD_B)
            dve.sem_inc(m_dve, LEAD_B)
            dve.sem_inc(k_diag_done, 2 * LEAD_B)
            dve.sem_inc(g_dve, len(G_DVE) * LEAD_B)
            dve.sem_inc(top_done, 8 * LEAD_B)

            def run(turn, s, stages):
                for step, n, b, p in stage_steps(X_DVE, turn, s, stages):
                    if step == "H":
                        dve.wait_ge(pe_g, done(b - 1, GT_H, NG))
                        dve.tensor_scalar(h2[:, :], xs[:, b, :], mv[:, b, 0:1], rstd[:, b, 0:1], ALU.subtract, ALU.mult).then_inc(h2_done, 1)
                        if stages == "A":
                            dve.memset(k_diag[:, :, :, :].bitcast(F32), 0.0).then_inc(k_diag_set, 1)
                    elif step == "KD":
                        dve.wait_ge(g_act, done(b, G_ACT[3 + n], len(G_ACT)))
                        dve.wait_ge(pe_l1, done(b - 1, 4 * n + 3, 8))
                        if stages == "A":
                            dve.wait_ge(k_diag_set, 1)
                        groups = slice(4 * n, 4 * n + 4)
                        for hl in range(4):
                            part = slice(hl * QUAD, hl * QUAD + 3 * XDIM)
                            ins = dve.tensor_copy(k_diag[part, groups, hl, :], kt[part, p, groups, :])
                        ins.then_inc(k_diag_done, 1)
                    elif step == "M":
                        dve.wait_ge(pe_m, done(b, 1, 2))
                        dve.wait_ge(pe_l2, done(b - 1, 7, 8))
                        if "C" not in stages:
                            dve.wait_ge(q_diag_set, 1)
                        for hl in (2, 3):
                            part = slice(hl * QUAD, hl * QUAD + 3 * XDIM + 1)
                            ins = dve.tensor_copy(q_diag[part, 4:8, hl, :], bank(ps_1[1], 0, 512, 4)[part])
                        ins.then_inc(m_dve, 1)
                    elif step == "G":
                        which = G_DVE[n]
                        ps = ps_g[n % 2][:, 0:DIM].rearrange("p (h c) -> p h c", c=XDIM)
                        dve.wait_ge(pe_g, done(b, n, NG))
                        if n == GT_KV:
                            dve.wait_ge(v_done, done(b))
                        dve.wait_ge(rot_done, done(b - 1, which, 2))
                        cos_b = cos[:, b, :, :].rearrange("p f c -> p (f c)").unsqueeze(1).to_broadcast([P, XHEADS, XDIM])
                        pairs = ps.rearrange("p h (f c) -> p h f c", c=2)
                        out2 = by_sin[:, which, :, :].rearrange("p h (f c) -> p h f c", c=2)
                        dve.tensor_tensor(by_cos[:, which, :, :], ps, cos_b, ALU.mult)
                        for c in range(2):
                            sin_b = sin[:, b, :, c].unsqueeze(1).to_broadcast([P, XHEADS, 4])
                            ins = dve.tensor_tensor(out2[:, :, :, c], pairs[:, :, :, 1 - c], sin_b, ALU.mult)
                        ins.then_inc(g_dve, 1)
                    elif step == "L1":
                        dve.wait_ge(pe_l1, done(b, n, 8))
                        dve.tensor_reduce(top[:, n, :], bank(ps_1[n % 2], 0, 512, 4), AX.X, ALU.max).then_inc(top_done, 1)
                    elif step == "NEG":
                        dve.wait_ge(top_done, done(b, 7, 8))
                        if "C" not in stages:
                            dve.wait_ge(set_done, 3)
                        dve.tensor_scalar(stack[:, 1 + p, :, 3 * XDIM].bitcast(F32R), top[:, :, :].rearrange("p g h -> p (g h)"), -1.0, None,
                                          ALU.mult).then_inc(neg_done, 1)
                    elif step == "DV":
                        av = (ps_av, ps_m)[n][:, :].rearrange("p (h c) -> p h c", c=QUAD)
                        heads = slice(16 * n, 16 * n + 16)
                        dve.wait_ge(pe_ab, done(b, n, 2))
                        dve.reciprocal(rsum[:, heads], av[:, :, XDIM]).then_inc(rsum_done, 1)
                        dve.wait_ge(rsum_done, done(b, n, 2))
                        dve.wait_ge(pe_at, done(b - 1))
                        dve.tensor_tensor(att[:, :].rearrange("p (h c) -> p h c", c=XDIM)[:, heads, :], av[:, :, 0:XDIM],
                                          rsum[:, heads].unsqueeze(2).to_broadcast([P, 16, XDIM]), ALU.mult).then_inc(att_done, 1)
                    elif step == "OUT":
                        dve.wait_ge(pe_out, done(b))
                        dve.wait_ge(bias_done, done(b))
                        dve.tensor_tensor(xs[:, b, :], ps_m[:, 0:DIM], xs[:, b, :], ALU.add).then_inc(added, 1)
                    elif step == "S3":
                        dve.wait_ge(added, done(b))
                        dve.sem_inc(waited, 1)
                        dve.bn_stats(out=stats3[:, :], in_=xs[:, b, :]).then_inc(stats3_done, 1)
                        dve.wait_ge(stats3_done, done(b))
                        dve.wait_ge(hn_done, done(b - 1))
                        dve.sem_inc(waited, 1)
                        dve.bn_aggr(out=mv3[:, :], in_=stats3[:, :]).then_inc(mv3_done, 1)
                        dve.wait_ge(mv3_done, done(b))
                        dve.wait_ge(rstd3_done, done(b - 1))
                        dve.tensor_scalar(var_eps3[:, :], mv3[:, 1:2], EPS, None, ALU.add).then_inc(var3_done, 1)
                    elif step == "HN":
                        dve.wait_ge(rstd3_done, done(b))
                        dve.tensor_scalar(hn[:, b, :], xs[:, b, :], mv3[:, 0:1], rstd3[:, 0:1], ALU.subtract, ALU.mult).then_inc(hn_done, 1)

            sequences(dve, run)

        @block.scalar
        def _(act):
            act.sem_inc(g_act, len(G_ACT) * LEAD_B)
            act.sem_inc(exp_done, 8 * LEAD_B)
            act.sem_inc(v_done, LEAD_B)
            act.sem_inc(hi_done, 2 * LEAD_B)
            act.sem_inc(att_t_done, LEAD_B)
            act.sem_inc(m_act, 2 * LEAD_B)
            act.sem_inc(avt_done, 2 * LEAD_B)

            def high_of_expert(e):
                act.activation(w["w13_hi"][:, :, e, :], w["w13_raw"][:, :, e, :], ACT.Copy).then_inc(w["w_hi_done"], 1)

            def run(turn, s, stages):
                for step, n, b, p in stage_steps(X_ACT, turn, s, stages):
                    if step == "L2":
                        act.wait_ge(pe_l2, done(b, n, 8))
                        act.wait_ge(pe_av, done(b, n - 2, 8) if n >= 2 else done(b - 1, n + 6, 8))
                        act.activation(wt[:, n % 2, :, :], bank(ps_2[n % 2], 0, 512, 4), ACT.Exp, scale=XDIM ** -0.5).then_inc(exp_done, 1)
                    elif step == "V":
                        act.wait_ge(pe_g, done(b, GT_KV, NG))
                        act.wait_ge(pe_av, done(b - 3, 7, 8))
                        if "C" not in stages:
                            act.wait_ge(set_done, 1)
                        act.activation(va[:, p, 0:XHEADS * XV].rearrange("p (h c) -> p h c", c=XV)[:, :, 0:XDIM], ps_g[0][:, DIM:2 * DIM].rearrange("p (h c) -> p h c", c=XDIM),
                                       ACT.Copy).then_inc(v_done, 1)
                    elif step == "G" and n == GT_H:
                        act.wait_ge(pe_g, done(b, n, NG))
                        act.wait_ge(pe_g, done(b - 1, GT_Q, NG))
                        act.activation(h2t[:, :, :], bank(ps_g[1], 0, DIM, KC), ACT.Copy).then_inc(g_act, 1)
                    elif step == "G":
                        act.wait_ge(pe_g, done(b, n, NG))
                        ps = bank(ps_g[n % 2], 0, 512, 4)
                        if n < GT_QT:
                            act.wait_ge(pe_l2, done(b - 3, 7, 8))
                            ins = act.activation(kt[:, p, 4 * (n - 3):4 * (n - 2), :], ps, ACT.Copy)
                        else:
                            act.wait_ge(pe_l1, done(b - 1, 7, 8))
                            ins = act.activation(qt[:, 4 * (n - 5):4 * (n - 4), :], ps, ACT.Copy)
                        ins.then_inc(g_act, 1)
                    elif step == "M":
                        act.wait_ge(pe_m, done(b, n, 2))
                        if n == 0:
                            act.wait_ge(pe_l2, done(b - 1, 7, 8))
                            if "C" not in stages:
                                act.wait_ge(q_diag_set, 1)
                        for hl in ((0, 1, 2, 3), (0, 1))[n]:
                            part = slice(hl * QUAD, hl * QUAD + 3 * XDIM + 1)
                            ins = act.activation(q_diag[part, 4 * n:4 * n + 4, hl, :], bank(ps_1[n], 0, 512, 4)[part], ACT.Copy)
                        ins.then_inc(m_act, 1)
                    elif step == "HI":
                        act.wait_ge(rot_done, done(b, n, 2))
                        if n == 0:
                            act.wait_ge(pe_g, done(b - 1, 4, NG))
                        else:
                            act.wait_ge(pe_m, done(b - 3, 1, 2))
                        for at_ in ((0, 1), (0, 2))[n]:
                            ins = act.activation(stack[:, (0, 1 + p)[n], :, at_ * XDIM:(at_ + 1) * XDIM].bitcast(F32R), rot[:, n, :, :], ACT.Copy)
                        ins.then_inc(hi_done, 1)
                    elif step == "AC":
                        act.wait_ge(pe_av, done(b, 4 * n + 3, 8))
                        act.wait_ge(pe_ab, done(b - 1, n, 2))
                        act.activation(avt[:, n, :, :], bank((ps_av, ps_m)[n], 0, 512, 4), ACT.Copy).then_inc(avt_done, 1)
                    elif step == "AT":
                        act.wait_ge(pe_at, done(b))
                        act.wait_ge(pe_out, done(b - 1))
                        act.activation(att_t[:, :, :], bank(ps_m, 0, DIM, KC), ACT.Copy).then_inc(att_t_done, 1)
                    elif step == "SPLIT":
                        high_of_expert(b + 1)
                if stages == "A":
                    act.wait_ge(w["w13_in"], 16)
                    high_of_expert(0)

            act.preload_act_table_set("natural_log_exp_and_others")
            sequences(act, run)

        @block.gpsimd
        def _(pool):
            for s, k in ((rstd3_done, 1), (ctx_done, 1), (rot_done, 2), (lo_done, 2), (bias_done, 1)):
                pool.sem_inc(s, k * LEAD_B)
            pool.memset(minus_half[:, :], -0.5).then_inc(half_set, 1)
            pool.wait_ge(half_set, 1)

            def low_of_expert(e):
                pool.wait_ge(w["w_hi_done"], e + 1)
                pool.tensor_tensor(w["w13_lo"][:, :, e, :], w["w13_raw"][:, :, e, :], w["w13_hi"][:, :, e, :].bitcast(F32), ALU.subtract)

            def run(turn, s, stages):
                for step, n, b, p in stage_steps(X_POOL, turn, s, stages):
                    if step == "CTX":
                        if stages == "A":
                            pool.wait_ge(ctx_in, 16)
                        pool.wait_ge(pe_g, done(b - 1, GT_KV, NG))
                        pool.tensor_copy(ctx_b[:, :], ctx_all[:, b, :]).then_inc(ctx_done, 1)
                        if stages == "A":
                            pool.memset(va[:, :, :], 1.0).then_inc(set_done, 1)
                            pool.memset(stack[:, 1:4, :, 3 * XDIM:], 0.0).then_inc(set_done, 1)
                            pool.memset(stack[:, 0, :, 3 * XDIM:], 1.0).then_inc(set_done, 1)
                    elif step == "ROT":
                        pool.wait_ge(g_dve, done(b, n, len(G_DVE)))
                        pool.wait_ge(lo_done, done(b - 1, n, 2))
                        pool.tensor_tensor(rot[:, n, :, :], by_cos[:, n, :, :], by_sin[:, n, :, :], ALU.add).then_inc(rot_done, 1)
                    elif step == "LO":
                        pool.wait_ge(hi_done, done(b, n, 2))
                        lo = (2, 1)[n]
                        which = (0, 1 + p)[n]
                        pool.tensor_tensor(stack[:, which, :, lo * XDIM:(lo + 1) * XDIM].bitcast(F32R), rot[:, n, :, :],
                                           stack[:, which, :, 0:XDIM], ALU.subtract).then_inc(lo_done, 1)
                    elif step == "S3":
                        pool.wait_ge(var3_done, done(b))
                        pool.wait_ge(hn_done, done(b - 1))
                        pool.tensor_tensor(rstd3[:, :], var_eps3[:, :], minus_half[:, 0:1], ALU.pow).then_inc(rstd3_done, 1)
                    elif step == "SPLIT":
                        low_of_expert(b + 1)
                    elif step == "BIAS":
                        if stages == "A":
                            pool.wait_ge(bout_in, 16)
                        pool.wait_ge(h2_done, done(b))
                        pool.tensor_tensor(xs[:, b, :], xs[:, b, :], bout[:, :], ALU.add).then_inc(bias_done, 1)

                if stages == "A":
                    pool.memset(q_diag[:, :, :, :].bitcast(F32), 0.0).then_inc(q_diag_set, 1)
                    low_of_expert(0)

            sequences(pool, run)


EXPERTS, HID, TOPK = 8, 128, 2
NE = EXPERTS + 1


def feed_forward(nc, banks, xs, hn, ht_hi, ht_lo, con, w, a, out):
    ident = con[:, C_ID:C_ID + P]

    with ExitStack() as ctx:
        def sb(name, shape, dt=F32):
            return ctx.enter_context(nc.sbuf_tensor("ff_" + name, shape, dt))

        def sem(name):
            return ctx.enter_context(nc.semaphore("ff_" + name))

        one_plus, score = sb("one_plus", [P, SEQS, EXPERTS]), sb("score", [P, SEQS, EXPERTS])
        above, same = sb("above", [P, SEQS, EXPERTS, EXPERTS]), sb("same", [P, SEQS, EXPERTS, EXPERTS])
        rank, scale = sb("rank", [P, SEQS, EXPERTS]), sb("scale", [P, NE, SEQS])
        act_out, hid, hid_t = sb("act_out", [P, 2, HID]), sb("hid", [P, 2, HID]), sb("hid_t", [P, 2, TOK], F32R)
        hid_t_lo, w2_hi, w2_lo = sb("hid_t_lo", [P, 2, TOK], F32R), sb("w2_hi", [P, NE, DIM], F32R), sb("w2_lo", [P, NE, DIM], F32R)

        norm = Norm(nc, ctx, banks, xs, hn, ht_hi, ht_lo, ident, "norm3")
        ones_set, routed, exp_done, step_done, scale_done = [sem(n) for n in ("ones_set", "routed", "exp_done", "step_done", "scale_done")]
        up, silu_done, hid_done, turned, hid_t_done, down, added, stored = [
            sem(n) for n in ("up", "silu_done", "hid_done", "turned", "hid_t_done", "down", "added", "stored")]
        gate_hi_done, gate_lo_done = sem("gate_hi_done"), sem("gate_lo_done")
        route_t, routed_t, route_t_done = sb("route_t", [EXPERTS, 2, HALF]), sem("routed_t"), sem("route_t_done")
        w2_hi_done, w2_lo_done, hid_t_lo_done = sem("w2_hi_done"), sem("w2_lo_done"), sem("hid_t_lo_done")

        ps_u, ps_t, ps_y = banks[0:2], banks[2:4], banks[4:8]
        ps_r, ps_rt = banks[4], banks[5:7]
        block = ctx.enter_context(nc.Block())

        def tile(t, b):
            return SEQS * t + b + 1

        @block.sync
        def _(sp):
            for c in range(4):
                sp.wait_ge(added, c + 1)
                sp.dma_start(out[2 * c:2 * c + 2].rearrange("b t d -> t b d"), xs[:, 2 * c:2 * c + 2, :]).then_inc(stored, 16)
            sp.wait_ge(stored, 4 * 16)

        @block.tensor
        def _(pe):
            norm.tensor(pe, normalised_here=False)
            pe.wait_ge(gate_lo_done, 1)

            def route(half):
                pe.wait_ge(norm.lo_done, 2 * half + 2)
                cols = slice(half * HALF, (half + 1) * HALF)
                for kc in range(KC):
                    mm = split_product(pe, ps_rt[half][0:EXPERTS, :], w["gate_hi"][:, kc, :], w["gate_lo"][:, kc, :],
                                       ht_hi[:, kc, cols], ht_lo[:, kc, cols], kc == 0, kc == KC - 1)
                mm.then_inc(routed_t, 1)

            def route_back(half):
                pe.wait_ge(route_t_done, half + 1)
                for b in range(4):
                    at_ = (4 * half + b) * EXPERTS
                    mm = pe.transpose(ps_r[:, at_:at_ + EXPERTS], route_t[:, half, b * TOK:(b + 1) * TOK], ident[0:EXPERTS, 0:EXPERTS])
                mm.then_inc(routed, 1)

            def turn_over(t, b):
                pe.wait_ge(hid_done, tile(t, b))
                if not (isinstance(t, int) and t == 0 and b < 2):
                    pe.wait_ge(hid_t_lo_done, tile(t, b - 2))
                pe.transpose(ps_t[b % 2][:, 0:TOK], hid[:, b % 2, :], ident).then_inc(turned, 1)

            def project(t, b):
                if b == 0:
                    pe.wait_ge(w2_lo_done, t + 1)
                    if isinstance(t, int) and t == 0:
                        pe.wait_ge(exp_done, 1)
                pe.wait_ge(hid_t_lo_done, tile(t, b))
                out_b, first = ps_y[b // 2][:, b % 2 * DIM:(b % 2 + 1) * DIM], isinstance(t, int) and t == 0 and b % 2 == 0
                pe.matmul(out_b, hid_t[:, b % 2, :], w2_hi[:, t, :], start=first, stop=False, skip_group_check=True)
                pe.matmul(out_b, hid_t[:, b % 2, :], w2_lo[:, t, :], start=False, stop=False, skip_group_check=True)
                pe.matmul(out_b, hid_t_lo[:, b % 2, :], w2_hi[:, t, :], start=False, stop=False, skip_group_check=True).then_inc(down, 1)

            def run(t, first):
                for b in range(SEQS):
                    if first:
                        pe.wait_ge(norm.lo_done, b // 4 * 2 + 2)
                    if not first or b >= 2:
                        pe.wait_ge(hid_done, tile(t, b - 2))
                    for kc in range(KC):
                        mm = split_product(pe, ps_u[b % 2][:, 0:2 * HID], ht_hi[:, kc, b * TOK:(b + 1) * TOK],
                                           ht_lo[:, kc, b * TOK:(b + 1) * TOK], w["w13_hi"][:, kc, t, :], w["w13_lo"][:, kc, t, :],
                                           kc == 0, kc == KC - 1)
                    mm.then_inc(up, 1)
                    if first and b < 2:
                        route(b)
                    elif first and b < 4:
                        route_back(b - 2)
                    if b >= 2:
                        turn_over(t, b - 2)
                    elif not first:
                        turn_over(t - 1, b + 6)
                    if b >= 4:
                        project(t, b - 4)
                    elif not first:
                        project(t - 1, b + 4)

            run(0, True)
            run(1, False)
            with pe.Fori(2, NE) as t:
                run(t, False)
            turn_over(NE - 1, 6)
            project(NE - 1, 4)
            turn_over(NE - 1, 7)
            for b in (5, 6, 7):
                project(NE - 1, b)

        @block.vector
        def _(dve):
            dve.memset(scale[:, 0, :], 1.0).then_inc(ones_set, 1)
            dve.wait_ge(gate_hi_done, 1)
            dve.tensor_tensor(w["gate_lo"][:, :, :], w["gate_raw"][:, :, :], w["gate_hi"][:, :, :].bitcast(F32), ALU.subtract).then_inc(gate_lo_done, 1)
            norm.vector_low(dve)

            def hidden(t, b):
                dve.wait_ge(silu_done, tile(t, b))
                if not (isinstance(t, int) and t == 0 and b < 2):
                    dve.wait_ge(turned, tile(t, b - 2))
                dve.scalar_tensor_tensor(out=hid[:, b % 2, :], in0=ps_u[b % 2][:, HID:2 * HID], scalar=scale[:, t, b:b + 1],
                                         in1=act_out[:, b % 2, :], op0=ALU.mult, op1=ALU.mult).then_inc(hid_done, 1)

            def low(t, b):
                dve.wait_ge(hid_t_done, tile(t, b))
                dve.tensor_tensor(hid_t_lo[:, b % 2, :], ps_t[b % 2][:, 0:TOK], hid_t[:, b % 2, :].bitcast(F32),
                                  ALU.subtract).then_inc(hid_t_lo_done, 1)

            def run(t, first):
                for b in range(SEQS):
                    hidden(t, b)
                    if b >= 2:
                        low(t, b - 2)
                    elif not first:
                        low(t - 1, b + 6)
                    if first and 4 <= b < 7:
                        rank_piece(b - 4)
                if first:
                    dve.wait_ge(scale_done, 1)

            def link(ins, n):
                ins.then_inc(step_done, 1)
                dve.wait_ge(step_done, n)

            def compare(seqs):
                for b in seqs:
                    own = score[:, b, :].unsqueeze(2).to_broadcast([P, EXPERTS, EXPERTS])
                    other = score[:, b, :].unsqueeze(1).to_broadcast([P, EXPERTS, EXPERTS])
                    dve.tensor_tensor(above[:, b, :, :], other, own, ALU.is_gt)
                    ins = dve.tensor_tensor(same[:, b, :, :], other, own, ALU.is_equal)
                return ins

            def rank_piece(n):
                before = con[:, C_BEFORE:C_BEFORE + 64].unsqueeze(1).to_broadcast([P, SEQS, 64])
                flat = same[:, :, :, :].rearrange("p b e f -> p b (e f)")
                if n == 0:
                    dve.wait_ge(exp_done, 1)
                    link(dve.tensor_scalar(one_plus[:, :, :], one_plus[:, :, :], 1.0, None, ALU.add), 1)
                    link(dve.reciprocal(score[:, :, :], one_plus[:, :, :]), 2)
                    compare(range(4))
                elif n == 1:
                    link(compare(range(4, SEQS)), 3)
                    link(dve.tensor_tensor(flat, flat, before, ALU.mult), 4)
                    link(dve.tensor_tensor(above[:, :, :, :], above[:, :, :, :], same[:, :, :, :], ALU.add), 5)
                else:
                    link(dve.tensor_reduce(rank[:, :, :], above[:, :, :, :], AX.X, ALU.add), 6)
                    link(dve.tensor_scalar(rank[:, :, :], rank[:, :, :], TOPK - 0.5, None, ALU.is_lt), 7)
                    dve.tensor_tensor(scale[:, 1:NE, :].rearrange("p e b -> p b e"), rank[:, :, :], score[:, :, :], ALU.mult).then_inc(scale_done, 1)

            run(0, True)
            run(1, False)
            with dve.Fori(2, NE) as t:
                run(t, False)
            low(NE - 1, 6)
            low(NE - 1, 7)
            for c in range(4):
                dve.wait_ge(down, tile(NE - 1, 2 * c + 1))
                dve.tensor_tensor(xs[:, 2 * c:2 * c + 2, :], bank(ps_y[c], 0, 512, 2), xs[:, 2 * c:2 * c + 2, :], ALU.add).then_inc(added, 1)

        @block.scalar
        def _(act):
            act.wait_ge(w["gate_in"], 16)
            act.activation(w["gate_hi"][:, :, :], w["gate_raw"][:, :, :], ACT.Copy).then_inc(gate_hi_done, 1)
            norm.scalar(act)
            act.wait_ge(w["w2_in"], 16)

            def w2_high(e):
                act.activation(w2_hi[:, e, :], w["w2"][:, e, :], ACT.Copy).then_inc(w2_hi_done, 1)

            w2_high(0)

            def exponential():
                act.wait_ge(routed, 2)
                act.activation(one_plus[:, :, :], ps_r[:, 0:SEQS * EXPERTS].rearrange("p (b e) -> p b e", b=SEQS), ACT.Exp,
                               scale=-1.0).then_inc(exp_done, 1)

            def silu(t, b):
                act.wait_ge(up, tile(t, b))
                if not (isinstance(t, int) and t == 0 and b < 2):
                    act.wait_ge(hid_done, tile(t, b - 2))
                act.activation(act_out[:, b % 2, :], ps_u[b % 2][:, 0:HID], ACT.Silu, scale=scale[:, t, b:b + 1]).then_inc(silu_done, 1)

            def keep(t, b):
                act.wait_ge(turned, tile(t, b))
                if not (isinstance(t, int) and t == 0 and b < 2):
                    act.wait_ge(down, tile(t, b - 2))
                act.activation(hid_t[:, b % 2, :], ps_t[b % 2][:, 0:TOK], ACT.Copy).then_inc(hid_t_done, 1)

            def run(t, first):
                for b in range(SEQS):
                    silu(t, b)
                    if first:
                        w2_high(b + 1)
                    if first and b < 2:
                        act.wait_ge(routed_t, b + 1)
                        act.activation(route_t[:, b, :], ps_rt[b][0:EXPERTS, :], ACT.Copy).then_inc(route_t_done, 1)
                    if b >= 2:
                        keep(t, b - 2)
                    elif not first:
                        keep(t - 1, b + 6)
                    if first and b == 3:
                        exponential()

            act.wait_ge(ones_set, 1)
            run(0, True)
            act.wait_ge(scale_done, 1)
            run(1, False)
            with act.Fori(2, NE) as t:
                run(t, False)
            keep(NE - 1, 6)
            keep(NE - 1, 7)

        @block.gpsimd
        def _(pool):
            for e in range(NE):
                pool.wait_ge(w2_hi_done, e + 1)
                pool.tensor_tensor(w2_lo[:, e, :], w["w2"][:, e, :], w2_hi[:, e, :].bitcast(F32), ALU.subtract).then_inc(w2_lo_done, 1)


def decoder_layer(nc, a, out):
    with ExitStack() as ctx:
        def sb(name, shape, dt=F32):
            return ctx.enter_context(nc.sbuf_tensor(name, shape, dt))

        banks = [ctx.enter_context(nc.psum_tensor(f"bank{n}", [P, 512], F32)) for n in range(8)]
        xs = sb("xs", [P, SEQS, DIM])
        hn = sb("hn", [P, SEQS, DIM])
        ht_hi, ht_lo = sb("ht_hi", [P, KC, ALL], F32R), sb("ht_lo", [P, KC, ALL], F32R)
        con = sb("con", [P, C_ALL])
        x_in = [ctx.enter_context(nc.semaphore(f"x_in{n}")) for n in range(2)]
        rotary = Rotary(nc, ctx, con)
        early = dict(
            wkv=sb("wkv", [P, 2 * DIM]), ctx_all=sb("ctx_all", [P, SEQS, TOK]),
            par_in=ctx.enter_context(nc.semaphore("par_in")), ctx_in=ctx.enter_context(nc.semaphore("ctx_in")),
            mv=sb("mv", [P, SEQS, 2]), rstd=sb("rstd", [P, SEQS, 1]))
        slot_attention(nc, banks, xs, hn, ht_hi, ht_lo, con, rotary, early, x_in, a)

        w = dict(
            w13_raw=sb("w13_raw", [P, KC, NE, 2 * HID]), w13_hi=sb("w13_hi", [P, KC, NE, 2 * HID], F32R),
            w13_lo=sb("w13_lo", [P, KC, NE, 2 * HID], F32R), w2=sb("w2", [P, NE, DIM]),
            gate_raw=sb("gate_raw", [P, KC, EXPERTS]), gate_hi=sb("gate_hi", [P, KC, EXPERTS], F32R),
            gate_lo=sb("gate_lo", [P, KC, EXPERTS], F32R),
            w13_in=ctx.enter_context(nc.semaphore("w13_in")), gate_in=ctx.enter_context(nc.semaphore("gate_in")),
            w2_in=ctx.enter_context(nc.semaphore("w2_in")), w_hi_done=ctx.enter_context(nc.semaphore("w_hi_done")))
        cross_attention(nc, banks, xs, hn, con, rotary, early, w, a)
        feed_forward(nc, banks, xs, hn, ht_hi, ht_lo, con, w, a, out)


def layouts(i):
    def rows(m):
        return m.reshape(KC, P, -1).transpose(1, 0, 2)

    def heads(m):
        return rows(m).reshape(P, KC, PAIRS, 2, DK).transpose(2, 0, 1, 3, 4)

    q, k, v, g = (heads(i["L0_attn_" + n].T) for n in ("Wq", "Wk", "Wv", "Wg"))
    ws1 = np.zeros((P, KC, P), np.float32)
    ws2 = np.zeros((P, PAIRS, P), np.float32)
    for n in range(4):
        ws1[:, :, QUAD * n:QUAD * n + S_RANK] = rows(i["L0_attn_Ws1"].T)
        ws2[QUAD * n:QUAD * n + S_RANK] = i["L0_attn_Ws2"].T.reshape(S_RANK, PAIRS, P)
        ws2[QUAD * n + S_RANK] = i["L0_attn_bs2"].reshape(PAIRS, P)
    w1 = np.concatenate([i["L0_ffn_sw1"][None], i["L0_ffn_w1"]])
    w3 = np.concatenate([i["L0_ffn_sw3"][None], i["L0_ffn_w3"]])
    w2 = np.concatenate([i["L0_ffn_sw2"][None], i["L0_ffn_w2"]])
    return {
        "x": i["x"],
        "constants": constants(),
        "wqk": np.stack([q, k], axis=4).reshape(PAIRS, P, KC, 512),
        "wvg": np.stack([v, g], axis=3).reshape(PAIRS, P, KC, 512),
        "ws1": ws1,
        "ws2": ws2,
        "g_norm": i["L0_attn_g_norm_weight"].reshape(P, 1),
        "wo": i["L0_attn_Wo"].T.reshape(PAIRS, 2, P, DIM).transpose(0, 2, 1, 3),
        "pos": i["fside_BxSx2_0"],
        "ctx_t": i["ctx_1024"].transpose(0, 2, 1),
        "xwq": rows(i["L0_xattn_Wq"]),
        "wkv": i["L0_xattn_Wkv"],
        "wout": rows(i["L0_xattn_Wout"]),
        "bout": i["L0_xattn_bout"].reshape(1, DIM),
        "gate": rows(i["L0_ffn_gate_w"].T),
        "w13": np.stack([w1, w3], axis=1).reshape(NE * 2 * HID, DIM).T.reshape(KC, P, NE, 2 * HID).transpose(1, 0, 2, 3),
        "w2": w2.transpose(2, 0, 1),
    }


def kernel(**inputs):
    import numpy as _np
    import concourse.bacc as _bacc
    from concourse import mybir as _mybir
    from concourse.bass_utils import run_bass_kernel_spmd as _run

    nc = _bacc.Bacc("TRN2", target_bir_lowering=False, num_devices=1)
    arrays = {n: _np.ascontiguousarray(m) for n, m in layouts({n: _np.asarray(m) for n, m in inputs.items()}).items()}
    handles = {n: nc.dram_tensor(f"in_{n}", m.shape, _mybir.dt.from_np(m.dtype), kind="ExternalInput").ap() for n, m in arrays.items()}
    out = nc.dram_tensor("out", (SEQS, TOK, DIM), F32, kind="ExternalOutput").ap()
    decoder_layer(nc, handles, out)
    r = _run(nc, [{f"in_{n}": m for n, m in arrays.items()}], core_ids=[0])
    return r.results[0]["out"]
```
